# Optimizing a Trainium2 kernel written in Bass

```python
import numpy as np
import jax
import jax.numpy as jnp

def _softmax(x, axis=-1):
    return jax.nn.softmax(x, axis=axis)

def _gelu(x):
    return jax.nn.gelu(x, approximate=True)

def _silu(x):
    return jax.nn.silu(x)

def _sigmoid(x):
    return jax.nn.sigmoid(x)

def _layernorm(x, axis=-1, eps=1e-05):
    m = jnp.mean(x, axis=axis, keepdims=True)
    v = jnp.var(x, axis=axis, keepdims=True)
    return (x - m) / jnp.sqrt(v + eps)

def _scatter_add(tgt, idx, src, axis=0):
    return tgt.at[idx].add(src)

def _segment_sum(src, seg, n):
    return jax.ops.segment_sum(src, seg, n)
kernel_name = 'mk_macaron_d1_jaxref_r8_913695'

def setup_inputs(seed: int=0):
    np.random.seed(seed)
    _w = jnp.asarray

    def _L0_attn_setup():
        import jax, jax.numpy as jnp
        import numpy as np
        B, S, E, H = (2, 256, 512, 32)
        D = E // H
        ROPE_BASE = 10000.0
        MASK_VAL = -66504.0

        def _rope(x, cos, sin):
            x1, x2 = jnp.split(x, 2, axis=-1)
            return jnp.concatenate([x1 * cos - x2 * sin, x2 * cos + x1 * sin], axis=-1)
        key = jax.random.key(seed)
        k1, k2, k3, k4, k5 = jax.random.split(key, 5)
        return {'hidden_states': jax.random.normal(k1, (B, S, E), dtype=jnp.float32), 'qkv_w': jax.random.normal(k2, (E, 3 * E), dtype=jnp.float32) * 0.02, 'qkv_b': jax.random.normal(k3, (3 * E,), dtype=jnp.float32) * 0.02, 'out_w': jax.random.normal(k4, (E, E), dtype=jnp.float32) * 0.02, 'out_b': jax.random.normal(k5, (E,), dtype=jnp.float32) * 0.02}
    _L0_attn_in = _L0_attn_setup()

    def _L0_ffn_setup():
        import jax, jax.numpy as jnp
        import numpy as np
        BLOCK = 64
        NF4_CODE = jnp.array([-1.0, -0.6961928009986877, -0.5250730514526367, -0.39491748809814453, -0.28444138169288635, -0.18477343022823334, -0.09105003625154495, 0.0, 0.07958029955625534, 0.16093020141124725, 0.24611230194568634, 0.33791524171829224, 0.44070982933044434, 0.5626170039176941, 0.7229568362236023, 1.0], dtype=jnp.float32)

        def dequant_nf4(q, absmax, shape):
            w = NF4_CODE[q.reshape(-1)]
            w = w.reshape(-1, BLOCK) * absmax[:, None]
            return w.reshape(shape)
        key = jax.random.key(seed)
        ks = jax.random.split(key, 7)
        HD, M = (512, 1792)
        nblk = HD * M // BLOCK
        x = jax.random.normal(ks[0], (2, 256, HD), dtype=jnp.float32)
        gate_q = jax.random.randint(ks[1], (M, HD), 0, 16, dtype=jnp.int32)
        up_q = jax.random.randint(ks[2], (M, HD), 0, 16, dtype=jnp.int32)
        down_q = jax.random.randint(ks[3], (HD, M), 0, 16, dtype=jnp.int32)
        gate_absmax = jax.random.uniform(ks[4], (nblk,), dtype=jnp.float32) * 0.05
        up_absmax = jax.random.uniform(ks[5], (nblk,), dtype=jnp.float32) * 0.05
        down_absmax = jax.random.uniform(ks[6], (nblk,), dtype=jnp.float32) * 0.05
        return {'x': x, 'gate_q': gate_q, 'gate_absmax': gate_absmax, 'up_q': up_q, 'up_absmax': up_absmax, 'down_q': down_q, 'down_absmax': down_absmax}
    _L0_ffn_in = _L0_ffn_setup()
    _d = {'L0_attn_hidden_states': _L0_attn_in['hidden_states'], 'L0_attn_qkv_w': _L0_attn_in['qkv_w'], 'L0_attn_qkv_b': _L0_attn_in['qkv_b'], 'L0_attn_out_w': _L0_attn_in['out_w'], 'L0_attn_out_b': _L0_attn_in['out_b'], 'L0_ffn_gate_q': _L0_ffn_in['gate_q'], 'L0_ffn_gate_absmax': _L0_ffn_in['gate_absmax'], 'L0_ffn_up_q': _L0_ffn_in['up_q'], 'L0_ffn_up_absmax': _L0_ffn_in['up_absmax'], 'L0_ffn_down_q': _L0_ffn_in['down_q'], 'L0_ffn_down_absmax': _L0_ffn_in['down_absmax']}
    _x0 = _d['L0_attn_hidden_states']
    _d['L0_attn_hidden_states'] = jax.random.normal(jax.random.fold_in(jax.random.key(seed), 1), (1, 1024, 512), dtype=_x0.dtype)
    del _x0
    return _d

def reference(L0_attn_hidden_states, L0_attn_qkv_w, L0_attn_qkv_b, L0_attn_out_w, L0_attn_out_b, L0_ffn_gate_q, L0_ffn_gate_absmax, L0_ffn_up_q, L0_ffn_up_absmax, L0_ffn_down_q, L0_ffn_down_absmax):

    def _L0_attn_ref(hidden_states, qkv_w, qkv_b, out_w, out_b):
        import jax, jax.numpy as jnp
        import numpy as np
        B, S, E, H = (2, 256, 512, 32)
        D = E // H
        ROPE_BASE = 10000.0
        MASK_VAL = -66504.0

        def _rope(x, cos, sin):
            x1, x2 = jnp.split(x, 2, axis=-1)
            return jnp.concatenate([x1 * cos - x2 * sin, x2 * cos + x1 * sin], axis=-1)
        b, s, e = hidden_states.shape
        qkv = hidden_states @ qkv_w + qkv_b
        q, k, v = jnp.split(qkv, 3, axis=-1)
        q = q.reshape(b, s, H, D)
        k = k.reshape(b, s, H, D)
        v = v.reshape(b, s, H, D)
        half = D // 2
        inv_freq = 1.0 / ROPE_BASE ** (jnp.arange(0, half, dtype=jnp.float32) / half)
        ang = jnp.arange(s, dtype=jnp.float32)[:, None] * inv_freq[None, :]
        cos = jnp.cos(ang)[None, :, None, :]
        sin = jnp.sin(ang)[None, :, None, :]
        q = _rope(q, cos, sin)
        k = _rope(k, cos, sin)
        scale = 1.0 / jnp.sqrt(jnp.asarray(D, dtype=hidden_states.dtype))
        scores = jnp.einsum('bqhd,bkhd->bhqk', q, k) * scale
        causal = jnp.tril(jnp.ones((s, s), dtype=scores.dtype))
        scores = scores + (1.0 - causal) * MASK_VAL
        probs = jax.nn.softmax(scores, axis=-1)
        ctx = jnp.einsum('bhqk,bkhd->bqhd', probs, v).reshape(b, s, e)
        return ctx @ out_w + out_b

    def _L0_ffn_ref(x, gate_q, gate_absmax, up_q, up_absmax, down_q, down_absmax):
        import jax, jax.numpy as jnp
        import numpy as np
        BLOCK = 64
        NF4_CODE = jnp.array([-1.0, -0.6961928009986877, -0.5250730514526367, -0.39491748809814453, -0.28444138169288635, -0.18477343022823334, -0.09105003625154495, 0.0, 0.07958029955625534, 0.16093020141124725, 0.24611230194568634, 0.33791524171829224, 0.44070982933044434, 0.5626170039176941, 0.7229568362236023, 1.0], dtype=jnp.float32)

        def dequant_nf4(q, absmax, shape):
            w = NF4_CODE[q.reshape(-1)]
            w = w.reshape(-1, BLOCK) * absmax[:, None]
            return w.reshape(shape)
        HD = x.shape[-1]
        M = gate_q.shape[0]
        Wg = dequant_nf4(gate_q, gate_absmax, (M, HD))
        Wu = dequant_nf4(up_q, up_absmax, (M, HD))
        Wd = dequant_nf4(down_q, down_absmax, (HD, M))
        g = jnp.einsum('bsh,mh->bsm', x, Wg)
        u = jnp.einsum('bsh,mh->bsm', x, Wu)
        h = jax.nn.silu(g) * u
        return jnp.einsum('bsm,hm->bsh', h, Wd)
    x = L0_attn_hidden_states
    x = x + 0.5 * _L0_ffn_ref(_layernorm(x, axis=-1), L0_ffn_gate_q, L0_ffn_gate_absmax, L0_ffn_up_q, L0_ffn_up_absmax, L0_ffn_down_q, L0_ffn_down_absmax)
    x = x + _L0_attn_ref(_layernorm(x, axis=-1), L0_attn_qkv_w, L0_attn_qkv_b, L0_attn_out_w, L0_attn_out_b)
    x = x + 0.5 * _L0_ffn_ref(_layernorm(x, axis=-1), L0_ffn_gate_q, L0_ffn_gate_absmax, L0_ffn_up_q, L0_ffn_up_absmax, L0_ffn_down_q, L0_ffn_down_absmax)
    return x

_drawn_inputs = setup_inputs


def setup_inputs(seed=0):
    import zlib

    import numpy as np

    out = dict(_drawn_inputs(seed))
    spreads = {}
    factors = {'L0_attn_qkv_w': 3.388,
     'L0_attn_qkv_b': 6.299,
     'L0_attn_out_w': 2.967,
     'L0_attn_out_b': 2.888,
     'L0_ffn_gate_absmax': 3.003,
     'L0_ffn_up_absmax': 3.021,
     'L0_ffn_down_absmax': 3.028}
    for name, (base, spread) in spreads.items():
        noise = np.random.default_rng([zlib.crc32(name.encode()), seed]).standard_normal(out[name].shape)
        drawn = base * np.exp(spread * noise) if base else spread * noise
        out[name] = jnp.asarray(drawn.astype(out[name].dtype))
    for name, factor in factors.items():
        out[name] = (out[name] * factor).astype(out[name].dtype)
    return out
```

```python
from contextlib import ExitStack

import concourse.bass as bass
from concourse import mybir
from concourse.alu_op_type import AluOpType as ALU

ACT = mybir.ActivationFunctionType
AX = mybir.AxisListType
F32 = mybir.dt.float32
F32R = mybir.dt.float32r
BF16 = mybir.dt.bfloat16
I32 = mybir.dt.int32

P = 128
BANK = 512
HALF = 512
NF4_BLOCK = 64
HEADS = 32
EPS = 1e-5
MASKED = -66560.0 * 4
CREDIT = 2

NF4_LINES = {
    "n01": (0.30380716919898987, 1.1266502141952515),
    "n23": (0.1301555633544922, 0.12570475041866302),
    "n45": (0.09966795146465302, 0.014562468975782394),
    "p89": (0.08134990185499191, -0.0017696027643978596),
    "p1011": (0.0918029323220253, -0.029296500608325005),
    "p1213": (0.12190717458724976, -0.16882605850696564),
    "p1415": (0.2770431637763977, -1.2163453102111816),
}
NF4_SLOPE_67 = 0.09105003625154495
LINE_ORDER = ["p1011", "p1213", "n23", "n45", "p1415", "n01", "p89"]
LINE_SLOT = {name: n for n, name in enumerate(LINE_ORDER)}
LINES = len(LINE_ORDER)
MERGES = 6


def macaron_block(nc, x, qkv_w, qkv_b, out_w, out_b, gate_q, gate_absmax, up_q, up_absmax,
                  down_q, down_absmax, rope_cos, rope_sin, identity, out):
    S, E = x.shape[1], x.shape[2]
    M = gate_q.shape[0]
    ST = S // P
    HT = ST // 2
    KT = E // P
    MT = M // P
    DU = MT // 2
    UNITS = MT + DU
    CALL_UNITS = MT + 2 * DU
    D = E // HEADS
    GH = 4
    GROUPS = HEADS // GH
    GW = GH * D
    SLOT = 64
    KA = 3 * D
    KB = KA + 2

    with ExitStack() as top:
        def sem(name):
            return top.enter_context(nc.semaphore(name))

        def sb(ctx, name, shape, dt):
            return ctx.enter_context(nc.sbuf_tensor(name, shape, dt))

        xres = sb(top, "xres", [P, ST, E], F32)
        ident = sb(top, "ident", [P, P], F32)
        causal_mask = sb(top, "causal_mask", [P, S], BF16)
        cos_t = sb(top, "cos_t", [P, ST, D], F32)
        sin_t = sb(top, "sin_t", [P, ST, D], F32)
        absmax_gu = sb(top, "absmax_gu", [P, 2, MT, E // NF4_BLOCK], F32)
        absmax_d = sb(top, "absmax_d", [P, KT, M // NF4_BLOCK], F32)
        qkv_bias = sb(top, "qkv_bias", [P, 3 * E], F32)
        out_bias = sb(top, "out_bias", [P, E], F32)
        xn = sb(top, "xn", [P, 2, E], F32)
        stats = sb(top, "stats", [P, ST, 6], F32)
        moments = sb(top, "moments", [P, ST, 2], F32)
        minus_half = sb(top, "minus_half", [P, HT], F32)
        rstd_tmp = sb(top, "rstd_tmp", [P, 5, HT], F32)
        rstd = sb(top, "rstd", [P, ST], F32)

        with ExitStack() as ffn_mem:
            lines = sb(ffn_mem, "lines", [P, LINES, 1024], F32)
            xT_hi = sb(ffn_mem, "xT_hi", [P, KT, S], F32R)
            xT_lo = sb(ffn_mem, "xT_lo", [P, KT, S], F32R)
            codes = [sb(ffn_mem, f"codes{n}", [P, 1024], I32) for n in range(2)]
            t_code = sb(ffn_mem, "t_code", [P, 2, 1024], BF16)
            t_neg = sb(ffn_mem, "t_neg", [P, 2, 1024], BF16)
            w_scaled = sb(ffn_mem, "w_scaled", [P, 1024], F32)
            wT = [sb(ffn_mem, f"wT{n}", [P, 2, 1024], F32R) for n in range(2)]
            hs = [sb(ffn_mem, f"hs{n}", [P, 2, 2, HALF], F32R) for n in range(2)]
            silu_g = sb(ffn_mem, "silu_g", [P, 2, HALF], F32)
            hid = sb(ffn_mem, "hid", [P, MT, S], F32)

        with ExitStack() as proj_mem:
            raw_w = sb(proj_mem, "raw_w", [P, KT, 3 * E], F32)
            wqkv = [sb(proj_mem, f"wqkv_{part}", [P, KT, 3 * E], F32R) for part in ("hi", "lo")]
            xs = [sb(proj_mem, f"xs_{part}", [P, 2, KT, P], F32R) for part in ("hi", "lo")]
            q_biased = sb(proj_mem, "q_biased", [P, E], F32)
            k_biased = sb(proj_mem, "k_biased", [P, E], F32)
            q_swapped = sb(proj_mem, "q_swapped", [P, E], F32)
            k_swapped = sb(proj_mem, "k_swapped", [P, E], F32)

        with ExitStack() as attn_mem:
            stack_q = sb(attn_mem, "stack_q", [P, ST, GH, SLOT], F32)
            stack_k = sb(attn_mem, "stack_k", [P, ST, GH, SLOT], F32)
            qT = [sb(attn_mem, f"qT{n}", [P, 2, S], F32R) for n in range(2)]
            qTm = [sb(attn_mem, f"qTm{n}", [P, 2, S], F32R) for n in range(2)]
            kT = [sb(attn_mem, f"kT{n}", [P, 2, S], F32R) for n in range(2)]
            probs = [[sb(attn_mem, f"probs{a}{b}", [P, 2, HALF], F32) for b in range(2)] for a in range(2)]
            v_ext = [sb(attn_mem, f"v_ext{n}", [P, ST, GH, 32], F32) for n in range(2)]
            ctxT = sb(attn_mem, "ctxT", [P, HALF], F32)
            masked = sb(attn_mem, "masked", [P, 2, BANK], BF16)
            maxima = sb(attn_mem, "maxima", [P, 2, ST, GH], F32)
            row_max = sb(attn_mem, "row_max", [P, ST, GH], F32)
            inv_den = sb(attn_mem, "inv_den", [P, 2, HT, GH], F32)
            q_nat = sb(attn_mem, "q_nat", [P, ST, E], F32)
            k_nat = sb(attn_mem, "k_nat", [P, ST, E], F32)
            v_nat = sb(attn_mem, "v_nat", [P, ST, E], F32)
            ctx_nat = sb(attn_mem, "ctx_nat", [P, ST, E], F32)
            wo = [sb(attn_mem, f"wo_{part}", [P, KT, E], F32R) for part in ("hi", "lo")]

        ps = top.enter_context(nc.psum_tensor("ps", [P, 8, BANK], F32))

        scratch = nc.dram_tensor("weights_split", (UNITS, P, 2, 1024), F32, kind="Internal").ap()

        x_loaded = [sem(f"x_loaded{n}") for n in range(2)]
        consts_loaded = sem("consts_loaded")
        codes_loaded = [sem(f"codes_loaded{n}") for n in range(2)]
        t_ready = sem("t_ready")
        t_neg_ready = sem("t_neg_ready")
        lines_ready = sem("lines_ready")
        merged = sem("merged")
        summed = sem("summed")
        w_ready = sem("w_ready")
        w_turned = sem("w_turned")
        hi_ready = sem("hi_ready")
        lo_ready = sem("lo_ready")
        spilled = [sem(f"spilled{n}") for n in range(2)]
        reloaded = [sem(f"reloaded{n}") for n in range(2)]
        down_used = sem("down_used")
        gate_done = sem("gate_done")
        up_done = sem("up_done")
        silu_done = sem("silu_done")
        hid_done = sem("hid_done")
        hs_hi_ready = sem("hs_hi_ready")
        hs_ready = sem("hs_ready")
        x_updated = sem("x_updated")
        const_set = sem("const_set")
        maxima_set = sem("maxima_set")
        waits_passed = sem("waits_passed")
        norm_stats = sem("norm_stats")
        norm_moments = sem("norm_moments")
        rstd_step = sem("rstd_step")
        rstd_ready = sem("rstd_ready")
        xn_ready = sem("xn_ready")
        xn_turned = sem("xn_turned")
        xT_hi_ready = sem("xT_hi_ready")
        xT_ready = sem("xT_ready")
        stored = sem("stored")
        raw_loaded = [sem("wqkv_loaded"), sem("wo_loaded")]
        raw_hi = sem("raw_hi")
        raw_split = sem("raw_split")
        xs_used = sem("xs_used")
        qkv_taken = sem("qkv_taken")
        qk_biased = sem("qk_biased")
        k_rope = sem("k_rope")
        q_rope = sem("q_rope")
        pads_set = sem("pads_set")
        stack_hi = sem("stack_hi")
        stack_ready = sem("stack_ready")
        v_staged = sem("v_staged")
        turned = sem("turned")
        turn_taken = {"act": sem("turn_taken_act"), "dve": sem("turn_taken_dve")}
        max_scored = sem("max_scored")
        max_taken = sem("max_taken")
        row_max_step = sem("row_max_step")
        max_stacked = sem("max_stacked")
        scored = sem("scored")
        exp_done = sem("exp_done")
        diag_masked = sem("diag_masked")
        pv_done = sem("pv_done")
        ctxT_taken = sem("ctxT_taken")
        inverted = sem("inverted")
        ctx_turned = sem("ctx_turned")
        ctx_hi = sem("ctx_hi")
        ctx_lo = sem("ctx_lo")
        projected = sem("projected")
        bias_added = sem("bias_added")
        x_attended = sem("x_attended")

        PV_STEPS = [(half, kt) for half in range(2) for kt in range((half + 1) * HT)]
        NPV = len(PV_STEPS)
        DIAG = [kt * P >= half * HALF for half, kt in PV_STEPS]
        NDIAG = sum(DIAG)

        def first_col(half, kt):
            return max(0, kt * P - half * HALF)

        MAX_TILES = [(st, j, c, min((st + 1) * P - c, BANK))
                     for st in range(ST) for j in range(GH) for c in range(0, (st + 1) * P, BANK)]
        NMAX = len(MAX_TILES)

        def next_group_work():
            work = [[] for _ in range(NPV)]
            work[1] += [("turn", n) for n in range(4)]
            work[2] += [("turn", n) for n in range(4, 8)]
            per = -(-NMAX // 7)
            for n in range(NMAX):
                work[3 + n // per].append(("max", n))
            work[NPV - 2].append(("stack_max", 0))
            work[NPV - 1] += [("turn", n) for n in range(8, 12)]
            return work

        def group_plan(this, following):
            work = next_group_work() if following else [[]] * NPV
            plan = [("stack", 0)] if following else []
            for n in range(NPV):
                if this:
                    plan += [("score", 2 * n), ("score", 2 * n + 1)]
                plan += work[n]
                if this and n >= 1:
                    plan.append(("pv", n - 1))
                    if n - 1 == HT - 1:
                        plan.append(("take_ctx", 0))
                    if n - 1 == HT + 1:
                        plan.append(("turn_ctx", 0))
            if this:
                plan += [("pv", NPV - 1), ("take_ctx", 1), ("turn_ctx", 1)]
            return plan

        def turn_engine(kind, n):
            return "dve" if kind == "turn_ctx" or n % 2 else "act"

        def turns_of(plan):
            return [turn_engine(*e) for e in plan if e[0] in ("turn", "turn_ctx")]

        FIRST_PLAN, BODY_PLAN, LAST_PLAN = group_plan(False, True), group_plan(True, True), group_plan(True, False)
        FIRST_TURNS, BODY_TURNS = turns_of(FIRST_PLAN), turns_of(BODY_PLAN)

        def wait_apart(eng, signal, count):
            eng.wait_ge(signal, count)
            eng.sem_inc(waits_passed, 1)

        def leading(g):
            return isinstance(g, int) and g < 0

        def turns_before(g, engine=None):
            def of(turns):
                return len([e for e in turns if engine in (None, e)])

            return 0 if leading(g) else of(FIRST_TURNS) + of(BODY_TURNS) * g

        TURN_BANK, PV_BANK, MAX_BANK = 5, 4, 6

        def run_groups(eng, run_plan):
            run_plan(FIRST_PLAN, -1, 1)
            with eng.Fori(0, GROUPS // 2 - 1) as i:
                for u in range(2):
                    run_plan(BODY_PLAN, 2 * i + u, u)
            run_plan(BODY_PLAN, GROUPS - 2, 0)
            run_plan(LAST_PLAN, GROUPS - 1, 1)

        x_dram = x[0].rearrange("(t p) e -> p t e", p=P)
        out_dram = out[0].rearrange("(t p) e -> p t e", p=P)
        down_dram = down_q.rearrange("(c p) m -> p c m", p=P)

        CONSTS = 8

        def wait_unit_free(eng, call, n):
            if isinstance(n, int) and n >= MT + 2:
                eng.wait_ge(down_used, 2 * DU * call + n - MT - 1)
            elif isinstance(n, int) and n < 2 and call > 0:
                eng.wait_ge(down_used, 2 * DU * call + n - 1)
            else:
                eng.wait_ge(up_done, 2 * MT * call + 2 * n + 2)

        def reload_count(v):
            first = UNITS + (v - UNITS) % 2
            return (v - first) // 2 + 1

        def rope(eng, nat, biased, swapped, st, ready, steps):
            dst = nat[:, bass.ds(st, 1), :].rearrange("p a (h t d) -> p (a h) t d", t=2, d=D // 2)
            src = biased[:, :].rearrange("p (h t d) -> p h t d", t=2, d=D // 2)
            tmp = swapped[:, :].rearrange("p (h t d) -> p h t d", t=2, d=D // 2)
            cos, sin = (tab[:, bass.ds(st, 1), :].rearrange("p a (t d) -> p a t d", t=2)
                        .broadcast_to([P, HEADS, 2, D // 2]) for tab in (cos_t, sin_t))
            wait_apart(eng, *ready)
            eng.tensor_tensor(dst, src, cos, ALU.mult).then_inc(steps, 1)
            eng.tensor_tensor(tmp, src[:, :, ::-1, :], sin, ALU.mult).then_inc(steps, 1)
            wait_apart(eng, steps, 3 * st + 3)
            eng.tensor_tensor(dst, dst, tmp, ALU.add).then_inc(steps, 1)

        def take_turn(eng, n, u):
            dst = (kT, qT, qTm)[n // 4][u][:, n % 4 // 2, n % 2 * HALF:(n % 2 + 1) * HALF]
            if eng is nc.scalar:
                eng.activation(dst, ps[:, TURN_BANK, :], ACT.Copy).then_inc(turn_taken["act"], 1)
            else:
                eng.tensor_copy(dst, ps[:, TURN_BANK, :]).then_inc(turn_taken["dve"], 1)

        block = top.enter_context(nc.Block())

        @block.sync
        def _(sp):
            def load_gate_up(s, u, k):
                cv = codes[u][:, :].rearrange("p (a e) -> p a e", a=2)
                sp.dma_start(cv[:, 0:1, :], gate_q.rearrange("(t p) e -> p t e", p=P)[:, bass.ds(s, 1), :]
                             ).then_inc(codes_loaded[u], 16)
                sp.dma_start(cv[:, 1:2, :], up_q.rearrange("(t p) e -> p t e", p=P)[:, bass.ds(s, 1), :]
                             ).then_inc(codes_loaded[u], 16)

            def load_down(p, u):
                cv = codes[u][:, :].rearrange("p (c m) -> p c m", c=KT)
                for c in range(0, KT, 2):
                    sp.dma_start(cv[:, c:c + 2, :], down_dram[:, c:c + 2, bass.ds(2 * P * p, 2 * P)]
                                 ).then_inc(codes_loaded[u], 16)

            def spill(s, u):
                sp.wait_ge(lo_ready, s + 2)
                sp.dma_start(scratch[bass.ds(s, 1)].rearrange("a p h n -> (a p) h n"), wT[u][:, :, :].bitcast(F32)
                             ).then_inc(spilled[u], 16)

            def reload(s, call, n, u):
                wait_unit_free(sp, call, n)
                sp.dma_start(wT[u][:, :, :].bitcast(F32), scratch[bass.ds(s, 1)].rearrange("a p h n -> (a p) h n")
                             ).then_inc(reloaded[u], 16)

            for n in range(2):
                sp.sem_inc(spilled[n], 16)
            sp.dma_start(xres[:, 0:HT, :], x_dram[:, 0:HT, :]).then_inc(x_loaded[0], 16)
            load_gate_up(0, 0, 1)
            sp.dma_start(ident[:, :], identity).then_inc(consts_loaded, 16)
            sp.dma_start(absmax_gu[:, 0], gate_absmax.rearrange("(t p b) -> p t b", p=P, t=MT)).then_inc(consts_loaded, 16)
            sp.dma_start(absmax_gu[:, 1], up_absmax.rearrange("(t p b) -> p t b", p=P, t=MT)).then_inc(consts_loaded, 16)
            sp.dma_start(absmax_d[:, :, :], down_absmax.rearrange("(c p b) -> p c b", p=P, c=KT)).then_inc(consts_loaded, 16)
            sp.dma_start(xres[:, HT:ST, :], x_dram[:, HT:ST, :]).then_inc(x_loaded[1], 16)
            sp.dma_start(cos_t[:, :, :], rope_cos.rearrange("(t p) d -> p t d", p=P)).then_inc(consts_loaded, 16)
            sp.dma_start(sin_t[:, :, :], rope_sin.rearrange("(t p) d -> p t d", p=P)).then_inc(consts_loaded, 16)
            sp.dma_start(qkv_bias[:, :], qkv_b.rearrange("(a n) -> a n", a=1).broadcast_to([P, 3 * E])).then_inc(consts_loaded, 16)
            sp.dma_start(out_bias[:, :], out_b.rearrange("(a n) -> a n", a=1).broadcast_to([P, E])).then_inc(consts_loaded, 16)
            load_gate_up(1, 1, 1)
            with sp.Fori(0, MT // 2 - 1) as i:
                for u in range(2):
                    s = 2 * i + u
                    sp.wait_ge(t_ready, s + 1)
                    load_gate_up(s + 2, u, i + 2)
                    spill(s, u)
            for s in range(MT - 2, UNITS):
                if s + 2 < UNITS:
                    sp.wait_ge(t_ready, s + 1)
                    load_down(s + 2 - MT, s % 2)
                spill(s, s % 2)
            for n in range(2):
                sp.wait_ge(spilled[n], 16 + 16 * ((UNITS + 1 - n) // 2))
            sp.wait_ge(summed, UNITS + 1)
            sp.dma_start(raw_w[:, :, :], qkv_w.rearrange("(c p) n -> p c n", p=P)).then_inc(raw_loaded[0], 16)
            for p in range(DU):
                reload(MT + p, 0, UNITS + p, (UNITS + p) % 2)
            sp.wait_ge(raw_split, KT)
            sp.dma_start(raw_w[:, :, 0:E], out_w.rearrange("(c p) n -> p c n", p=P)).then_inc(raw_loaded[1], 16)

            sp.wait_ge(projected, ST + CREDIT)
            for n in range(2):
                reload(n, 1, n, n)
            with sp.Fori(0, MT // 2 - 1) as i:
                for u in range(2):
                    reload(2 * i + u + 2, 1, 2 * i + u + 2, u)
            for p in range(DU):
                reload(MT + p, 1, MT + p, (MT + p) % 2)
            for p in range(DU):
                reload(MT + p, 1, UNITS + p, (UNITS + p) % 2)

            sp.wait_ge(x_updated, 2 * ST)
            sp.dma_start(out_dram, xres[:, :, :]).then_inc(stored, 16)
            sp.wait_ge(stored, 16)

        @block.gpsimd
        def _(pool):
            def shift_codes(s, u, k):
                wait_apart(pool, codes_loaded[u], 32 * k)
                pool.tensor_scalar(t_code[:, u, :], codes[u][:, :], 1.0, -7.0, ALU.mult, ALU.add).then_inc(t_ready, 1)

            def scale_unit(s, absmax, shape):
                pool.wait_ge(merged, MERGES * (s + 2))
                pool.wait_ge(w_turned, s + 1)
                pool.tensor_tensor(w_scaled[:, :], lines[:, LINE_SLOT["n01"], :], lines[:, LINE_SLOT["p89"], :],
                                   ALU.add).then_inc(summed, 1)
                pool.wait_ge(summed, s + 2)
                wv = w_scaled[:, :].rearrange("p (a b n) -> p a b n", a=shape[0], b=shape[1])
                pool.tensor_tensor(wv, wv, absmax.unsqueeze(3).broadcast_to([P, *shape, NF4_BLOCK]),
                                   ALU.mult).then_inc(w_ready, 1)

            def scale_gate_up(s):
                scale_unit(s, absmax_gu[:, :, bass.ds(s, 1), :].rearrange("p a t b -> p a (t b)"), (2, E // NF4_BLOCK))

            def scale_down(s):
                scale_unit(s, absmax_d[:, :, bass.ds(4 * (s - MT), 4)], (KT, 2 * P // NF4_BLOCK))

            def inverse_deviation(half, first):
                pool.wait_ge(norm_moments, first + ST // 2 * (half + 1))
                a, b = half * HT, (half + 1) * HT
                base = rstd_steps[0]

                def step(ins):
                    rstd_steps[0] += 1
                    ins.then_inc(rstd_step, 1)
                    pool.wait_ge(rstd_step, rstd_steps[0])

                ve, r, rr, c = (rstd_tmp[:, n, :] for n in range(4))
                step(pool.tensor_scalar(ve, moments[:, a:b, 1], 1.0, EPS, ALU.mult, ALU.add))
                step(pool.tensor_tensor(r, ve, minus_half[:, :], ALU.pow))
                step(pool.tensor_tensor(rr, r, r, ALU.mult))
                step(pool.tensor_tensor(c, rr, ve, ALU.mult))
                step(pool.tensor_scalar(rr, c, -0.5, 1.5, ALU.mult, ALU.add))
                pool.tensor_tensor(rstd[:, a:b], r, rr, ALU.mult).then_inc(rstd_ready, 1)

            rstd_steps = [0]
            pool.memset(minus_half[:, :], -0.5).then_inc(const_set, 1)
            pool.memset(causal_mask[:, :], 0.0).then_inc(const_set, 1)
            pool.wait_ge(const_set, 2)
            pool.affine_select(out=causal_mask[:, S - P:S], in_=causal_mask[:, S - P:S], compare_op=ALU.is_ge,
                               fill=MASKED, base=0, pattern=[[-1, P]], channel_multiplier=1).then_inc(const_set, 1)
            pool.sem_inc(summed, 1)
            pool.wait_ge(const_set, 3)
            shift_codes(0, 0, 1)
            shift_codes(1, 1, 1)
            inverse_deviation(0, 0)
            inverse_deviation(1, 0)
            pool.wait_ge(consts_loaded, 16 * CONSTS)
            with pool.Fori(0, MT // 2 - 1) as i:
                for u in range(2):
                    scale_gate_up(2 * i + u)
                    shift_codes(2 * i + u + 2, u, i + 2)
            for s in range(MT - 2, UNITS):
                (scale_gate_up if s < MT else scale_down)(s)
                if s + 2 < UNITS:
                    shift_codes(s + 2, s % 2, (s + 2) // 2 + 1)

            for half in range(2):
                inverse_deviation(half, ST)

            pool.sem_inc(q_rope, 1)
            with pool.Fori(0, ST) as st:
                rope(pool, q_nat, q_biased, q_swapped, st, (qk_biased, 2 * st + 1), q_rope)

            pool.wait_ge(xs_used, ST + CREDIT)
            pool.wait_ge(k_rope, 3 * ST + 1)
            pool.wait_ge(q_rope, 3 * ST + 1)
            pool.wait_ge(raw_split, KT + 1)
            pool.memset(stack_k[:, :, :, KA:KB], 1.0).then_inc(pads_set, 1)
            pool.memset(stack_k[:, :, :, KB:SLOT], 0.0).then_inc(pads_set, 1)
            pool.memset(stack_q[:, :, :, KA:SLOT], 0.0).then_inc(pads_set, 1)
            for n in range(2):
                pool.memset(v_ext[n][:, :, :, D:D + 1], 1.0).then_inc(pads_set, 1)
                pool.memset(v_ext[n][:, :, :, D + 1:32], 0.0).then_inc(pads_set, 1)

            def attend(plan, g, u):
                diag = 0
                for kind, n in plan:
                    if kind == "stack":
                        cols = bass.ds((g + 1) * GW, GW)
                        qg = q_nat[:, :, cols].rearrange("p t (j d) -> p t j d", j=GH)
                        kg = k_nat[:, :, cols].rearrange("p t (j d) -> p t j d", j=GH)
                        wait_apart(pool, stack_hi, 2 * (g + 1) + 1)
                        pool.tensor_tensor(stack_q[:, :, :, D:2 * D], qg, stack_q[:, :, :, 0:D], ALU.subtract
                                           ).then_inc(stack_ready, 1)
                        pool.tensor_scalar(stack_q[:, :, :, 2 * D:3 * D], stack_q[:, :, :, 0:D], 1.0, 0.0, ALU.mult,
                                           ALU.add).then_inc(stack_ready, 1)
                        wait_apart(pool, stack_hi, 2 * (g + 1) + 2)
                        pool.tensor_scalar(stack_k[:, :, :, D:2 * D], stack_k[:, :, :, 0:D], 1.0, 0.0, ALU.mult,
                                           ALU.add).then_inc(stack_ready, 1)
                        pool.tensor_tensor(stack_k[:, :, :, 2 * D:3 * D], kg, stack_k[:, :, :, 0:D], ALU.subtract
                                           ).then_inc(stack_ready, 1)
                    if kind == "score" and DIAG[n // 2]:
                        half, kt = PV_STEPS[n // 2]
                        c = first_col(half, kt)
                        tile = probs[n // 2 % 2][n % 2][:, :, c:c + P]
                        wait_apart(pool, exp_done, 2 * NPV * g + n + 1 + CREDIT)
                        pool.affine_select(out=tile, in_=tile, compare_op=ALU.is_ge, fill=0.0, base=0,
                                           pattern=[[0, 2], [1, P]], channel_multiplier=-1).then_inc(diag_masked, 1)

            run_groups(pool, attend)

            pool.wait_ge(consts_loaded, 16 * CONSTS)
            for half in range(2):
                inverse_deviation(half, 2 * ST)

        @block.scalar
        def _(act):
            def line(name, s, u, src):
                a, b = NF4_LINES[name]
                act.activation(lines[:, LINE_SLOT[name], :], src[:, u, :], ACT.Copy, bias=b, scale=a).then_inc(lines_ready, 1)

            def lines_first(s, u):
                act.wait_ge(t_ready, s + 1)
                act.wait_ge(merged, MERGES * s + 1)
                line("p1011", s, u, t_code)
                act.wait_ge(merged, MERGES * s + 3)
                line("p1213", s, u, t_code)
                act.wait_ge(t_neg_ready, s + 1)
                line("n23", s, u, t_neg)
                act.wait_ge(merged, MERGES * s + 5)
                line("n45", s, u, t_neg)

            def lines_last(s, u):
                act.wait_ge(merged, MERGES * s + 6)
                line("p1415", s, u, t_code)
                act.wait_ge(summed, s + 1)
                line("n01", s, u, t_neg)
                line("p89", s, u, t_code)

            def split_hi(s, u, k):
                act.wait_ge(w_turned, s + 2)
                wait_unit_free(act, 0, s)
                act.wait_ge(spilled[u], 16 * k)
                act.activation(wT[u][:, 0, :].rearrange("p (a n) -> p a n", a=2), ps[:, 4:6, :], ACT.Copy
                               ).then_inc(hi_ready, 1)

            def silu(call, mt, half):
                n = 2 * MT * call + 2 * mt + half
                act.wait_ge(gate_done, n + 1)
                act.wait_ge(hid_done, n + 1)
                act.activation(silu_g[:, half, :], ps[:, 2 * half, :], ACT.Silu).then_inc(silu_done, 1)

            def hs_hi(call, n, u, half, p):
                wait_unit_free(act, call, n)
                act.activation(hs[u][:, 0, :, :], hid[:, bass.ds(2 * p, 2), half * HALF:(half + 1) * HALF], ACT.Copy
                               ).then_inc(hs_hi_ready, 1)

            def norm_hi(n, st):
                act.wait_ge(xn_turned, n + 1)
                act.activation(xT_hi[:, :, st * P:(st + 1) * P], ps[:, 6 + n % 2, :].rearrange("p (k s) -> p k s", k=KT),
                               ACT.Copy).then_inc(xT_hi_ready, 1)

            act.sem_inc(exp_done, CREDIT)
            act.sem_inc(ctxT_taken, 1)
            act.preload_act_table(ACT.Silu)
            lines_first(0, 0)
            lines_last(0, 0)
            for st in range(HT):
                norm_hi(st, st)
            lines_first(1, 1)
            lines_last(1, 1)
            for st in range(HT, ST):
                norm_hi(st, st)
            split_hi(0, 0, 1)
            lines_first(2, 0)
            lines_last(2, 0)
            with act.Fori(0, MT // 2 - 1) as i:
                for w in range(2):
                    s, u = 2 * i + 1 + w, (1 + w) % 2
                    split_hi(s, u, i + 1 + w)
                    lines_first(s + 2, u)
                    silu(0, s - 1, 0)
                    lines_last(s + 2, u)
                    silu(0, s - 1, 1)
            for s in range(MT - 1, UNITS):
                u = s % 2
                split_hi(s, u, s // 2 + 1)
                if s + 2 < UNITS:
                    lines_first(s + 2, u)
                if s <= MT:
                    silu(0, s - 1, 0)
                if s + 2 < UNITS:
                    lines_last(s + 2, u)
                if s <= MT:
                    silu(0, s - 1, 1)
                if s == MT:
                    act.wait_ge(hid_done, 2 * MT + CREDIT)
                if s >= MT:
                    hs_hi(0, s, u, 0, s - MT)
            for p in range(DU):
                v = UNITS + p
                hs_hi(0, v, v % 2, 1, p)
                if 2 <= p < 2 + KT:
                    c = p - 2
                    act.wait_ge(raw_loaded[0], 16)
                    act.activation(wqkv[0][:, c, :], raw_w[:, c, :], ACT.Copy).then_inc(raw_hi, 1)

            with act.Fori(0, ST // 2) as i:
                for u in range(2):
                    st = 2 * i + u
                    act.wait_ge(xn_turned, ST + st + 1)
                    act.wait_ge(xs_used, st + 1)
                    act.activation(xs[0][:, u, :, :], ps[:, 6 + u, :].rearrange("p (k s) -> p k s", k=KT), ACT.Copy
                                   ).then_inc(xT_hi_ready, 1)
            act.wait_ge(raw_loaded[1], 16)
            act.activation(wo[0][:, :, :], raw_w[:, :, 0:E], ACT.Copy).then_inc(raw_hi, 1)

            act.preload_act_table(ACT.Exp)
            act.wait_ge(pads_set, 3)

            def attend(plan, g, u):
                turn = 0
                for kind, n in plan:
                    if kind == "stack":
                        act.wait_ge(turned, turns_before(g))
                        cols = bass.ds((g + 1) * GW, GW)
                        for nat, stack in ((q_nat, stack_q), (k_nat, stack_k)):
                            act.activation(stack[:, :, :, 0:D].bitcast(F32R),
                                           nat[:, :, cols].rearrange("p t (j d) -> p t j d", j=GH), ACT.Copy
                                           ).then_inc(stack_hi, 1)
                    if kind in ("turn", "turn_ctx"):
                        if turn_engine(kind, n) == "act":
                            act.wait_ge(turned, turns_before(g) + turn + 1)
                            take_turn(nc.scalar, n, 1 - u)
                        turn += 1
                    if kind == "score":
                        half, kt = PV_STEPS[n // 2]
                        c = first_col(half, kt)
                        act.wait_ge(scored, 2 * NPV * g + n + 1)
                        act.wait_ge(pv_done, NPV * g + n // 2 + 1)
                        act.activation(probs[n // 2 % 2][n % 2][:, :, c:HALF], ps[:, 2 * (n % 2):2 * (n % 2) + 2, c:HALF],
                                       ACT.Exp, scale=float(D) ** -0.5).then_inc(exp_done, 1)
                    if kind == "take_ctx":
                        act.wait_ge(pv_done, NPV * g + CREDIT + (NPV if n else HT))
                        act.wait_ge(turned, turns_before(g) + (turn if n else 0))
                        act.activation(ctxT[:, :], ps[:, PV_BANK, :], ACT.Copy).then_inc(ctxT_taken, 1)

            run_groups(act, attend)

            with act.Fori(0, ST // 2) as i:
                for u in range(2):
                    st = 2 * i + u
                    act.wait_ge(ctx_turned, st + 1)
                    act.wait_ge(projected, st + 1)
                    act.activation(xs[0][:, u, :, :], ps[:, 2 + u, :].rearrange("p (k s) -> p k s", k=KT), ACT.Copy
                                   ).then_inc(ctx_hi, 1)

            act.preload_act_table(ACT.Silu)
            for st in range(ST):
                norm_hi(2 * ST + st, st)
            with act.Fori(0, MT) as mt:
                for half in range(2):
                    silu(1, mt, half)
            act.wait_ge(hid_done, 4 * MT + CREDIT)
            for half in range(2):
                for p in range(DU):
                    n = MT + DU * half + p
                    hs_hi(1, n, n % 2, half, p)

        @block.vector
        def _(dve):
            def slot(name):
                return lines[:, LINE_SLOT[name], :]

            def clamp_codes(s, u):
                dve.wait_ge(t_ready, s + 1)
                dve.tensor_scalar(t_neg[:, u, :], t_code[:, u, :], 0.0, None, ALU.min).then_inc(t_neg_ready, 1)

            def own(s, k):
                dve.wait_ge(merged, MERGES * (s + 1) + k)

            def merge_first(s):
                dve.wait_ge(lines_ready, LINES * s + 2)
                dve.tensor_tensor(slot("p1213"), slot("p1011"), slot("p1213"), ALU.max).then_inc(merged, 1)
                dve.wait_ge(lines_ready, LINES * s + 4)
                dve.tensor_tensor(slot("n45"), slot("n23"), slot("n45"), ALU.min).then_inc(merged, 1)

            def merge_last(s, u):
                dve.wait_ge(lines_ready, LINES * s + 5)
                own(s, 1)
                dve.tensor_tensor(slot("p1415"), slot("p1213"), slot("p1415"), ALU.max).then_inc(merged, 1)
                dve.wait_ge(lines_ready, LINES * s + 6)
                own(s, 2)
                dve.tensor_tensor(slot("n45"), slot("n01"), slot("n45"), ALU.min).then_inc(merged, 1)
                own(s, 4)
                dve.scalar_tensor_tensor(slot("n01"), t_neg[:, u, :], NF4_SLOPE_67, slot("n45"), ALU.mult, ALU.min
                                         ).then_inc(merged, 1)
                dve.wait_ge(lines_ready, LINES * s + 7)
                own(s, 3)
                dve.scalar_tensor_tensor(slot("p89"), slot("p1415"), 0.0, slot("p89"), ALU.max, ALU.max
                                         ).then_inc(merged, 1)

            def split_lo(s, u):
                dve.wait_ge(hi_ready, s + 1)
                dve.tensor_tensor(wT[u][:, 1, :].rearrange("p (a n) -> p a n", a=2), ps[:, 4:6, :],
                                  wT[u][:, 0, :].rearrange("p (a n) -> p a n", a=2).bitcast(F32), ALU.subtract
                                  ).then_inc(lo_ready, 1)

            def hidden(call, mt, half):
                n = 2 * MT * call + 2 * mt + half
                dve.wait_ge(silu_done, n + 1)
                dve.wait_ge(up_done, n + 5)
                dve.tensor_tensor(hid[:, bass.ds(mt, 1), half * HALF:(half + 1) * HALF].rearrange("p a n -> p (a n)"),
                                  silu_g[:, half, :], ps[:, 2 * half + 1, :], ALU.mult).then_inc(hid_done, 1)

            def hs_lo(k, u, half, p):
                dve.wait_ge(hs_hi_ready, k)
                dve.tensor_tensor(hs[u][:, 1, :, :], hid[:, bass.ds(2 * p, 2), half * HALF:(half + 1) * HALF],
                                  hs[u][:, 0, :, :].bitcast(F32), ALU.subtract).then_inc(hs_ready, 1)

            def add_down(n, half):
                dve.wait_ge(down_used, DU * (n + 1))
                for t in range(HT):
                    st = half * HT + t
                    dve.scalar_tensor_tensor(xres[:, st, :], ps[:, 4 * half + t, :], 0.5, xres[:, st, :],
                                             ALU.mult, ALU.add).then_inc(x_updated, 1)

            def norm_statistics(n0, half):
                for st in range(half * HT, (half + 1) * HT):
                    dve.bn_stats(stats[:, st, :], xres[:, st, :]).then_inc(norm_stats, 1)
                for st in range(half * HT, (half + 1) * HT):
                    dve.wait_ge(norm_stats, n0 + st + 1)
                    dve.bn_aggr(moments[:, st, :], stats[:, st, :]).then_inc(norm_moments, 1)

            def moments_of(st):
                return moments[:, bass.ds(st, 1), 0:1].rearrange("p a b -> p (a b)")

            def rstd_of(st):
                return rstd[:, bass.ds(st, 1)]

            def norm_half(n0, half):
                tiles = range(half * HT, (half + 1) * HT)
                norm_statistics(n0, half)
                dve.wait_ge(rstd_ready, n0 // HT + half + 1)

                def normalize(st):
                    dve.tensor_scalar(xn[:, st % 2, :], xres[:, st, :], moments[:, st, 0:1], rstd[:, st:st + 1],
                                      ALU.subtract, ALU.mult).then_inc(xn_ready, 1)

                def norm_lo(st):
                    dve.wait_ge(xT_hi_ready, n0 + st + 1)
                    dve.tensor_tensor(xT_lo[:, :, st * P:(st + 1) * P],
                                      ps[:, 6 + st % 2, :].rearrange("p (k s) -> p k s", k=KT),
                                      xT_hi[:, :, st * P:(st + 1) * P].bitcast(F32), ALU.subtract).then_inc(xT_ready, 1)

                normalize(tiles[0])
                for st in tiles:
                    if st + 1 in tiles:
                        normalize(st + 1)
                    norm_lo(st)

            dve.sem_inc(merged, MERGES)
            dve.sem_inc(lo_ready, 1)
            dve.sem_inc(hid_done, CREDIT)
            dve.sem_inc(qkv_taken, CREDIT)
            dve.sem_inc(max_taken, CREDIT)
            dve.sem_inc(max_stacked, 1)
            dve.sem_inc(k_rope, 1)
            clamp_codes(0, 0)
            clamp_codes(1, 1)
            dve.wait_ge(x_loaded[0], 16)
            norm_half(0, 0)
            merge_first(0)
            merge_last(0, 0)
            dve.wait_ge(x_loaded[1], 16)
            norm_half(0, 1)
            merge_first(1)
            merge_last(1, 1)
            split_lo(0, 0)
            clamp_codes(2, 0)
            merge_first(2)
            merge_last(2, 0)
            with dve.Fori(0, MT // 2 - 1) as i:
                for w in range(2):
                    s, u = 2 * i + 1 + w, (1 + w) % 2
                    split_lo(s, u)
                    clamp_codes(s + 2, u)
                    merge_first(s + 2)
                    hidden(0, s - 1, 0)
                    merge_last(s + 2, u)
                    hidden(0, s - 1, 1)
            for s in range(MT - 1, UNITS):
                u = s % 2
                split_lo(s, u)
                if s + 2 < UNITS:
                    clamp_codes(s + 2, u)
                    merge_first(s + 2)
                if s <= MT:
                    hidden(0, s - 1, 0)
                if s + 2 < UNITS:
                    merge_last(s + 2, u)
                if s <= MT:
                    hidden(0, s - 1, 1)
                if s >= MT:
                    hs_lo(s - MT + 1, u, 0, s - MT)
            add_down(0, 0)
            for p in range(DU):
                v = UNITS + p
                hs_lo(DU + p + 1, v % 2, 1, p)
                if 2 <= p < 2 + KT:
                    c = p - 2
                    dve.wait_ge(raw_hi, c + 1)
                    dve.tensor_tensor(wqkv[1][:, c, :], raw_w[:, c, :], wqkv[0][:, c, :].bitcast(F32), ALU.subtract
                                      ).then_inc(raw_split, 1)
            add_down(1, 1)

            for half in range(2):
                norm_statistics(ST, half)
            dve.wait_ge(rstd_ready, 4)
            dve.wait_ge(consts_loaded, 16 * CONSTS)

            def normalize_tile(st, u):
                dve.tensor_scalar(xn[:, u, :], xres[:, bass.ds(st, 1), :].rearrange("p a e -> p (a e)"),
                                  moments_of(st), rstd_of(st), ALU.subtract, ALU.mult).then_inc(xn_ready, 1)

            def tile_lo(st, u):
                dve.wait_ge(xT_hi_ready, ST + st + 1)
                dve.tensor_tensor(xs[1][:, u, :, :], ps[:, 6 + u, :].rearrange("p (k s) -> p k s", k=KT),
                                  xs[0][:, u, :, :].bitcast(F32), ALU.subtract).then_inc(xT_ready, 1)

            def take_qkv(st, u):
                dve.wait_ge(xs_used, st + 1 + CREDIT)
                dve.wait_ge(q_rope, 3 * st + 1)
                dve.tensor_tensor(q_biased[:, :], ps[:, 3 * u, :], qkv_bias[:, 0:E], ALU.add).then_inc(qk_biased, 1)
                dve.tensor_tensor(k_biased[:, :], ps[:, 3 * u + 1, :], qkv_bias[:, E:2 * E], ALU.add).then_inc(qk_biased, 1)
                dve.tensor_tensor(v_nat[:, bass.ds(st, 1), :].rearrange("p a e -> p (a e)"), ps[:, 3 * u + 2, :],
                                  qkv_bias[:, 2 * E:3 * E], ALU.add).then_inc(qkv_taken, 1)
                rope(dve, k_nat, k_biased, k_swapped, st, (qk_biased, 2 * st + 2), k_rope)

            normalize_tile(0, 0)
            normalize_tile(1, 1)
            tile_lo(0, 0)
            with dve.Fori(0, ST // 2 - 1) as i:
                for u in range(2):
                    st = 2 * i + u
                    normalize_tile(st + 2, u)
                    tile_lo(st + 1, 1 - u)
                    take_qkv(st, u)
            tile_lo(ST - 1, 1)
            take_qkv(ST - 2, 0)
            take_qkv(ST - 1, 1)
            dve.wait_ge(raw_hi, KT + 1)
            dve.tensor_tensor(wo[1][:, :, :], raw_w[:, :, 0:E], wo[0][:, :, :].bitcast(F32), ALU.subtract
                              ).then_inc(raw_split, 1)

            dve.wait_ge(xs_used, ST + CREDIT)
            dve.wait_ge(pads_set, 7)
            dve.memset(maxima[:, :, :, :], -3.0e38).then_inc(maxima_set, 1)
            dve.wait_ge(maxima_set, 1)
            dve.wait_ge(const_set, 3)

            def attend(plan, g, u):
                turn = 0
                for kind, n in plan:
                    if kind == "stack":
                        if not leading(g):
                            dve.wait_ge(pv_done, NPV * g + CREDIT)
                        dve.tensor_copy(v_ext[1 - u][:, :, :, 0:D],
                                        v_nat[:, :, bass.ds((g + 1) * GW, GW)].rearrange("p t (j d) -> p t j d", j=GH)
                                        ).then_inc(v_staged, 1)
                    if kind == "turn":
                        if turn_engine(kind, n) == "dve":
                            dve.wait_ge(turned, turns_before(g) + turn + 1)
                            take_turn(nc.vector, n, 1 - u)
                        turn += 1
                    if kind == "max":
                        st, j, c, width = MAX_TILES[n]
                        wait_apart(dve, max_scored, NMAX * (g + 1) + n + 1)
                        at = S - (st + 1) * P + c
                        dve.tensor_tensor_reduce(out=masked[:, n % 2, 0:width], in0=ps[:, MAX_BANK + n % 2, 0:width],
                                                 in1=causal_mask[:, at:at + width], scale=1.0, scalar=-3.0e38,
                                                 op0=ALU.add, op1=ALU.max,
                                                 accum_out=maxima[:, c // BANK, st, j:j + 1]).then_inc(max_taken, 1)
                    if kind == "stack_max":
                        dve.wait_ge(max_taken, NMAX * (g + 2) + CREDIT)
                        dve.tensor_tensor(row_max[:, :, :], maxima[:, 0], maxima[:, 1], ALU.max).then_inc(row_max_step, 1)
                        dve.wait_ge(row_max_step, g + 2)
                        dve.wait_ge(turned, turns_before(g) + turn)
                        dve.tensor_scalar(stack_q[:, :, :, KA].bitcast(F32R), row_max[:, :, :], -1.0, None, ALU.mult
                                          ).then_inc(max_stacked, 1)
                        dve.wait_ge(max_stacked, 2 * (g + 1) + 1 + 1)
                        dve.scalar_tensor_tensor(stack_q[:, :, :, KA + 1], row_max[:, :, :], -1.0, stack_q[:, :, :, KA],
                                                 ALU.mult, ALU.subtract).then_inc(max_stacked, 1)
                    if kind == "turn_ctx":
                        dve.wait_ge(turned, turns_before(g) + turn + 1)
                        tile = ps[:, TURN_BANK, :].rearrange("p (t j d) -> p t j d", t=HT, j=GH)
                        dve.reciprocal(inv_den[:, n, :, :], tile[:, :, :, D]).then_inc(inverted, 1)
                        dve.wait_ge(inverted, 2 * g + n + 1)
                        dve.tensor_tensor(ctx_nat[:, n * HT:(n + 1) * HT, bass.ds(g * GW, GW)]
                                          .rearrange("p t (j d) -> p t j d", j=GH), tile[:, :, :, 0:D],
                                          inv_den[:, n, :, :].unsqueeze(3).broadcast_to([P, HT, GH, D]), ALU.mult
                                          ).then_inc(turn_taken["dve"], 1)
                        turn += 1

            run_groups(dve, attend)

            dve.sem_inc(ctx_lo, CREDIT)
            dve.sem_inc(x_attended, CREDIT)

            def ctx_low(st, u):
                dve.wait_ge(ctx_hi, st + 1)
                dve.tensor_tensor(xs[1][:, u, :, :], ps[:, 2 + u, :].rearrange("p (k s) -> p k s", k=KT),
                                  xs[0][:, u, :, :].bitcast(F32), ALU.subtract).then_inc(ctx_lo, 1)

            def add_attended(st, u):
                xt = xres[:, bass.ds(st, 1), :].rearrange("p a e -> p (a e)")
                dve.tensor_tensor(xt, xt, out_bias[:, :], ALU.add).then_inc(bias_added, 1)
                dve.wait_ge(bias_added, st + 1)
                dve.wait_ge(projected, st + 1 + CREDIT)
                dve.tensor_tensor(xt, xt, ps[:, u, :], ALU.add).then_inc(x_attended, 1)

            with dve.Fori(0, ST // 2) as i:
                for u in range(2):
                    ctx_low(2 * i + u, u)
                    add_attended(2 * i + u, u)

            dve.wait_ge(x_attended, ST + CREDIT)
            norm_half(2 * ST, 0)
            norm_half(2 * ST, 1)
            with dve.Fori(0, MT) as mt:
                for half in range(2):
                    hidden(1, mt, half)
            for half in range(2):
                for p in range(DU):
                    n = MT + DU * half + p
                    hs_lo(DU * (2 + half) + p + 1, n % 2, half, p)
                add_down(2 + half, half)

        @block.tensor
        def _(pe):
            def turn(s, src):
                pe.wait_ge(w_ready, s + 1)
                pe.wait_ge(lo_ready, s + 1)
                for b in range(8):
                    ins = pe.transpose(ps[:, 4 + b // 4, (b % 4) * P:(b % 4 + 1) * P], src(b), ident[:, :])
                ins.then_inc(w_turned, 1)

            def turn_gate_up(s):
                turn(s, lambda b: w_scaled[:, b * P:(b + 1) * P])

            def turn_down(s):
                wv = w_scaled[:, :].rearrange("p (c m) -> p c m", c=KT)
                turn(s, lambda b: wv[:, b % 4, (b // 4) * P:(b // 4 + 1) * P])

            def weights_ready(v, u, k):
                if k is None:
                    pe.wait_ge(lo_ready, v + 2)
                else:
                    pe.wait_ge(reloaded[u], 16 * k)

            def gate_up(call, mt, v, u, k=None):
                weights_ready(v, u, k)
                for half in range(2):
                    cols = slice(half * HALF, (half + 1) * HALF)
                    pe.wait_ge(hid_done, 2 * MT * call + 2 * mt + half + 1)
                    for g, done in ((0, gate_done), (1, up_done)):
                        bank = ps[:, 2 * half + g, :]
                        for kt in range(KT):
                            w = [wT[u][:, part, (4 * g + kt) * P:(4 * g + kt + 1) * P] for part in range(2)]
                            pe.matmul(bank, w[0], xT_hi[:, kt, cols], start=kt == 0, stop=False)
                            pe.matmul(bank, w[1], xT_hi[:, kt, cols], start=False, stop=False)
                            ins = pe.matmul(bank, w[0], xT_lo[:, kt, cols], start=False, stop=kt == KT - 1)
                        ins.then_inc(done, 1)

            def down(half, v, u, h, k, first, last):
                weights_ready(v, u, k)
                pe.wait_ge(hs_ready, h)
                for j in range(2):
                    for t in range(HT):
                        a = [hs[u][:, part, j, t * P:(t + 1) * P] for part in range(2)]
                        w = [wT[u][:, part, j * E:(j + 1) * E] for part in range(2)]
                        bank = ps[:, 4 * half + t, :]
                        pe.matmul(bank, a[0], w[0], start=first and j == 0, stop=False)
                        pe.matmul(bank, a[1], w[0], start=False, stop=False)
                        ins = pe.matmul(bank, a[0], w[1], start=False, stop=last and j == 1)
                ins.then_inc(down_used, 1)

            def norm_turn(n):
                pe.wait_ge(xn_ready, n + 1)
                if n >= 2:
                    pe.wait_ge(xT_ready, n - 1)
                for k in range(KT):
                    ins = pe.transpose(ps[:, 6 + n % 2, k * P:(k + 1) * P], xn[:, n % 2, k * P:(k + 1) * P], ident[:, :])
                ins.then_inc(xn_turned, 1)

            pe.sem_inc(w_turned, 1)
            pe.sem_inc(up_done, 4)
            pe.wait_ge(consts_loaded, 16 * CONSTS)
            for st in range(ST):
                norm_turn(st)
            turn_gate_up(0)
            pe.wait_ge(xT_ready, ST)
            with pe.Fori(0, MT // 2 - 1) as i:
                for w in range(2):
                    s, u = 2 * i + 1 + w, (1 + w) % 2
                    turn_gate_up(s)
                    gate_up(0, s - 1, s - 1, 1 - u)
            for s in range(MT - 1, UNITS):
                (turn_gate_up if s < MT else turn_down)(s)
                if s <= MT:
                    gate_up(0, s - 1, s - 1, (s - 1) % 2)
                else:
                    if s == MT + 1:
                        pe.wait_ge(hid_done, 2 * MT + CREDIT)
                    down(0, s - 1, (s - 1) % 2, s - MT, None, s == MT + 1, False)
            down(0, UNITS - 1, (UNITS - 1) % 2, DU, None, False, True)
            for p in range(DU):
                v = UNITS + p
                down(1, v, v % 2, DU + p + 1, reload_count(v), p == 0, p == DU - 1)

            pe.sem_inc(xs_used, CREDIT)
            pe.sem_inc(pv_done, CREDIT)

            def project(u, w, cols, banks, done):
                for b in range(cols // BANK):
                    c = slice(b * BANK, (b + 1) * BANK)
                    for kt in range(KT):
                        pe.matmul(ps[:, banks + b, :], xs[0][:, u, kt, :], w[0][:, kt, c], start=kt == 0, stop=False)
                        pe.matmul(ps[:, banks + b, :], xs[1][:, u, kt, :], w[0][:, kt, c], start=False, stop=False)
                        ins = pe.matmul(ps[:, banks + b, :], xs[0][:, u, kt, :], w[1][:, kt, c], start=False,
                                        stop=kt == KT - 1)
                ins.then_inc(done, 1)

            def turn_tile(st, u):
                pe.wait_ge(xn_ready, ST + st + 1)
                pe.wait_ge(xT_ready, ST + st - 1)
                for k in range(KT):
                    ins = pe.transpose(ps[:, 6 + u, k * P:(k + 1) * P], xn[:, u, k * P:(k + 1) * P], ident[:, :])
                ins.then_inc(xn_turned, 1)

            def project_qkv(st, u):
                pe.wait_ge(xT_ready, ST + st + 1)
                pe.wait_ge(qkv_taken, st + 1)
                project(u, wqkv, 3 * E, 3 * u, xs_used)

            turn_tile(0, 0)
            pe.wait_ge(raw_split, KT)
            pe.wait_ge(x_updated, ST)
            with pe.Fori(0, ST // 2 - 1) as i:
                for u in range(2):
                    turn_tile(2 * i + u + 1, 1 - u)
                    project_qkv(2 * i + u, u)
            turn_tile(ST - 1, 1)
            project_qkv(ST - 2, 0)
            project_qkv(ST - 1, 1)

            pe.wait_ge(qkv_taken, ST + CREDIT)

            def attend(plan, g, u):
                turn = 0
                order = turns_of(plan)

                def wait_taken(engine, count):
                    pe.wait_ge(turn_taken[engine], turns_before(g, engine) + count)

                def wait_turn_bank():
                    if turn or not leading(g):
                        engine = order[turn - 1] if turn else "dve"
                        wait_taken(engine, order[:turn].count(engine))

                for kind, n in plan:
                    if kind == "turn":
                        if n == 0:
                            pe.wait_ge(stack_ready, 4 * (g + 2))
                        if n == 8:
                            pe.wait_ge(max_stacked, 2 * (g + 2) + 1)
                        wait_turn_bank()
                        stack = stack_k if n < 4 else stack_q
                        for t in range(HT):
                            pair = n % 4 // 2
                            src = stack[:, n % 2 * HT + t, 2 * pair:2 * pair + 2, :].rearrange("p j d -> p (j d)")
                            ins = pe.transpose(ps[:, TURN_BANK, t * P:(t + 1) * P], src, ident[:, :])
                        ins.then_inc(turned, 1)
                        turn += 1
                    if kind == "max":
                        st, j, c, width = MAX_TILES[n]
                        r = slice(j % 2 * SLOT, j % 2 * SLOT + KA)
                        if n == 0:
                            for engine in turn_taken:
                                wait_taken(engine, order[:8].count(engine))
                        pe.wait_ge(max_taken, NMAX * (g + 1) + n + 1)
                        pe.matmul(ps[:, MAX_BANK + n % 2, 0:width], qT[1 - u][r, j // 2, st * P:(st + 1) * P],
                                  kT[1 - u][r, j // 2, c:c + width], start=True, stop=True,
                                  tile_position=(j % 2 * SLOT, 0)).then_inc(max_scored, 1)
                    if kind == "score":
                        half, kt = PV_STEPS[n // 2]
                        c = first_col(half, kt)
                        pair = n % 2
                        if n == 0:
                            for engine in turn_taken:
                                wait_taken(engine, 0)
                        pe.wait_ge(exp_done, 2 * NPV * g + n + 1)
                        for j in range(2):
                            r = slice(j * SLOT, j * SLOT + KB)
                            ins = pe.matmul(ps[:, 2 * pair + j, c:HALF], kT[u][r, pair, kt * P:(kt + 1) * P],
                                            qTm[u][r, pair, half * HALF + c:(half + 1) * HALF], start=True, stop=True,
                                            tile_position=(j * SLOT, 0))
                        ins.then_inc(scored, 1)
                    if kind == "pv":
                        half, kt = PV_STEPS[n]
                        c = first_col(half, kt)
                        if n == 0:
                            pe.wait_ge(v_staged, g + 1)
                        if kt == 0:
                            pe.wait_ge(ctxT_taken, 2 * g + half + 1)
                        if DIAG[n]:
                            pe.wait_ge(diag_masked, 2 * NDIAG * g + 2 * sum(DIAG[:n + 1]))
                        pe.wait_ge(exp_done, 2 * NPV * g + 2 * n + 2 + CREDIT)
                        for j in range(GH):
                            ins = pe.matmul(ps[32 * j:32 * (j + 1), PV_BANK, c:HALF], v_ext[u][:, kt, j, :],
                                            probs[n % 2][j // 2][:, j % 2, c:HALF], start=kt == 0,
                                            stop=kt == (half + 1) * HT - 1, tile_position=(0, 32 * j))
                        ins.then_inc(pv_done, 1)
                    if kind == "turn_ctx":
                        pe.wait_ge(ctxT_taken, 2 * g + n + 2)
                        wait_turn_bank()
                        for t in range(HT):
                            ins = pe.transpose(ps[:, TURN_BANK, t * P:(t + 1) * P], ctxT[:, t * P:(t + 1) * P], ident[:, :])
                        ins.then_inc(turned, 1)
                        turn += 1

            run_groups(pe, attend)

            def turn_ctx_tile(st, u):
                pe.wait_ge(ctx_lo, st + 1)
                for k in range(KT):
                    ins = pe.transpose(ps[:, 2 + u, k * P:(k + 1) * P], ctx_nat[:, st, k * P:(k + 1) * P], ident[:, :])
                ins.then_inc(ctx_turned, 1)

            pe.wait_ge(turn_taken["dve"], turns_before(GROUPS - 1, "dve") + 2)
            pe.wait_ge(raw_split, KT + 1)
            def project_context(st, u):
                pe.wait_ge(ctx_lo, st + 1 + CREDIT)
                pe.wait_ge(x_attended, st + 1)
                project(u, wo, E, u, projected)

            pe.sem_inc(projected, CREDIT)
            turn_ctx_tile(0, 0)
            for st in range(ST):
                if st + 1 < ST:
                    turn_ctx_tile(st + 1, (st + 1) % 2)
                project_context(st, st % 2)

            for st in range(ST):
                norm_turn(2 * ST + st)
            pe.wait_ge(xT_ready, 3 * ST)
            with pe.Fori(0, MT // 2) as i:
                for u in range(2):
                    gate_up(1, 2 * i + u, 2 * i + u, u, i + reload_count(CALL_UNITS + u))
            pe.wait_ge(hid_done, 4 * MT + CREDIT)
            for half in range(2):
                for p in range(DU):
                    n = MT + DU * half + p
                    down(half, n, n % 2, DU * (2 + half) + p + 1, reload_count(CALL_UNITS + n), p == 0, p == DU - 1)


_INPUTS = ["L0_attn_hidden_states", "L0_attn_qkv_w", "L0_attn_qkv_b", "L0_attn_out_w", "L0_attn_out_b",
           "L0_ffn_gate_q", "L0_ffn_gate_absmax", "L0_ffn_up_q", "L0_ffn_up_absmax", "L0_ffn_down_q",
           "L0_ffn_down_absmax"]


def _constants(seq, head_dim):
    import numpy as np
    half = head_dim // 2
    inv_freq = np.float32(1.0) / np.float32(10000.0) ** (np.arange(half, dtype=np.float32) / np.float32(half))
    ang = np.arange(seq, dtype=np.float32)[:, None] * inv_freq[None, :].astype(np.float32)
    cos, sin = np.cos(ang).astype(np.float32), np.sin(ang).astype(np.float32)
    return {
        "rope_cos": np.concatenate([cos, cos], 1),
        "rope_sin": np.concatenate([-sin, sin], 1),
        "identity": np.eye(P, dtype=np.float32),
    }


def kernel(**inputs):
    import numpy as np
    import concourse.bacc as bacc
    from concourse.bass_utils import run_bass_kernel_spmd

    nc = bacc.Bacc("TRN2", target_bir_lowering=False, num_devices=1)
    shape = inputs["L0_attn_hidden_states"].shape
    named = [(n, np.ascontiguousarray(inputs[n])) for n in _INPUTS]
    named += list(_constants(shape[1], shape[2] // HEADS).items())
    arrays, args = {}, []
    for name, a in named:
        arrays[f"in_{name}"] = a
        args.append(nc.dram_tensor(f"in_{name}", a.shape, mybir.dt.from_np(a.dtype), kind="ExternalInput").ap())
    args.append(nc.dram_tensor("out_0", shape, F32, kind="ExternalOutput").ap())
    macaron_block(nc, *args)
    r = run_bass_kernel_spmd(nc, [arrays], core_ids=[0])
    return r.results[0]["out_0"]
```

```python
from contextlib import ExitStack

import concourse.bass as bass
from concourse import mybir
from concourse.alu_op_type import AluOpType as ALU

ACT = mybir.ActivationFunctionType
AX = mybir.AxisListType
F32 = mybir.dt.float32
F32R = mybir.dt.float32r
BF16 = mybir.dt.bfloat16
I32 = mybir.dt.int32

P = 128
BANK = 512
HALF = 512
NF4_BLOCK = 64
HEADS = 32
EPS = 1e-5
MASKED = -66560.0 * 4
CREDIT = 2

NF4_LINES = {
    "n01": (0.30380716919898987, 1.1266502141952515),
    "n23": (0.1301555633544922, 0.12570475041866302),
    "n45": (0.09966795146465302, 0.014562468975782394),
    "p89": (0.08134990185499191, -0.0017696027643978596),
    "p1011": (0.0918029323220253, -0.029296500608325005),
    "p1213": (0.12190717458724976, -0.16882605850696564),
    "p1415": (0.2770431637763977, -1.2163453102111816),
}
NF4_SLOPE_67 = 0.09105003625154495
LINE_ORDER = ["p1011", "p1213", "n23", "n45", "p1415", "n01", "p89"]
LINE_SLOT = {name: n for n, name in enumerate(LINE_ORDER)}
LINES = len(LINE_ORDER)
MERGES = 6


def macaron_block(nc, x, qkv_w, qkv_b, out_w, out_b, gate_q, gate_absmax, up_q, up_absmax,
                  down_q, down_absmax, rope_cos, rope_sin, identity, out):
    S, E = x.shape[1], x.shape[2]
    M = gate_q.shape[0]
    ST = S // P
    HT = ST // 2
    KT = E // P
    MT = M // P
    DU = MT // 2
    UNITS = MT + DU
    CALL_UNITS = MT + 2 * DU
    D = E // HEADS
    GH = 4
    GROUPS = HEADS // GH
    GW = GH * D
    SLOT = 64
    KA = 3 * D
    SPACER = 1536
    KB = KA + 2

    with ExitStack() as top:
        def sem(name):
            return top.enter_context(nc.semaphore(name))

        def sb(ctx, name, shape, dt):
            return ctx.enter_context(nc.sbuf_tensor(name, shape, dt))

        xres = sb(top, "xres", [P, ST, E], F32)
        ident = sb(top, "ident", [P, P], F32)
        causal_mask = sb(top, "causal_mask", [P, P], BF16)
        ident_bf16 = sb(top, "ident_bf16", [P, P], BF16)
        cos_t = sb(top, "cos_t", [P, ST, D], F32)
        sin_t = sb(top, "sin_t", [P, ST, D], F32)
        absmax_gu = sb(top, "absmax_gu", [P, 2, MT, E // NF4_BLOCK], F32)
        absmax_d = sb(top, "absmax_d", [P, KT, M // NF4_BLOCK], F32)
        qkv_bias = sb(top, "qkv_bias", [P, 3 * E], F32)
        out_bias = sb(top, "out_bias", [P, E], F32)
        xn = sb(top, "xn", [P, 2, E], F32)
        stats = sb(top, "stats", [P, ST, 6], F32)
        moments = sb(top, "moments", [P, ST, 2], F32)
        minus_half = sb(top, "minus_half", [P, HT], F32)
        rstd_tmp = sb(top, "rstd_tmp", [P, 5, HT], F32)
        rstd = sb(top, "rstd", [P, ST], F32)

        with ExitStack() as ffn_mem:
            lines = sb(ffn_mem, "lines", [P, LINES, 1024], F32)
            xT_hi = sb(ffn_mem, "xT_hi", [P, KT, S], F32R)
            xT_lo = sb(ffn_mem, "xT_lo", [P, KT, S], F32R)
            codes = [sb(ffn_mem, f"codes{n}", [P, 1024], I32) for n in range(2)]
            t_code = sb(ffn_mem, "t_code", [P, 2, 1024], BF16)
            t_neg = sb(ffn_mem, "t_neg", [P, 2, 1024], BF16)
            w_scaled = sb(ffn_mem, "w_scaled", [P, 1024], F32)
            wT = [sb(ffn_mem, f"wT{n}", [P, 2, 1024], F32R) for n in range(2)]
            hs = [sb(ffn_mem, f"hs{n}", [P, 2, 2, HALF], F32R) for n in range(2)]
            silu_g = sb(ffn_mem, "silu_g", [P, 2, HALF], F32)
            hid = sb(ffn_mem, "hid", [P, MT, S], F32)

        with ExitStack() as proj_mem:
            raw_w = sb(proj_mem, "raw_w", [P, KT, 3 * E], F32)
            wqkv = [sb(proj_mem, f"wqkv_{part}", [P, KT, 3 * E], F32R) for part in ("hi", "lo")]
            xs = [sb(proj_mem, f"xs_{part}", [P, 2, KT, P], F32R) for part in ("hi", "lo")]
            q_biased = sb(proj_mem, "q_biased", [P, E], F32)
            k_biased = sb(proj_mem, "k_biased", [P, E], F32)
            q_swapped = sb(proj_mem, "q_swapped", [P, E], F32)
            k_swapped = sb(proj_mem, "k_swapped", [P, E], F32)

        with ExitStack() as attn_mem:
            stack_q = sb(attn_mem, "stack_q", [P, ST, GH, SLOT], F32)
            stack_k = sb(attn_mem, "stack_k", [P, ST, GH, SLOT], F32)
            qT = sb(attn_mem, "qT", [P, 2, S], F32R)
            qTm = [sb(attn_mem, f"qTm{n}", [P, 2, S], F32R) for n in range(2)]
            kT = [sb(attn_mem, f"kT{n}", [P, 2, S], F32R) for n in range(2)]
            probs = [[sb(attn_mem, f"probs{a}{b}", [P, 2, HALF], F32) for b in range(2)] for a in range(2)]
            v_ext = [sb(attn_mem, f"v_ext{n}", [P, ST, GH, 32], F32) for n in range(2)]
            ctxT = sb(attn_mem, "ctxT", [P, HALF], F32)
            maxima = sb(attn_mem, "maxima", [P, 2, ST, GH], F32)
            row_max = sb(attn_mem, "row_max", [P, ST, GH], F32)
            inv_den = sb(attn_mem, "inv_den", [P, 2, HT, GH], F32)
            sb(attn_mem, "spacer", [P, SPACER], F32)
            q_nat = sb(attn_mem, "q_nat", [P, ST, E], F32)
            k_nat = sb(attn_mem, "k_nat", [P, ST, E], F32)
            v_nat = sb(attn_mem, "v_nat", [P, ST, E], F32)
            ctx_nat = sb(attn_mem, "ctx_nat", [P, ST, E], F32)
            wo = [sb(attn_mem, f"wo_{part}", [P, KT, E], F32R) for part in ("hi", "lo")]

        ps = top.enter_context(nc.psum_tensor("ps", [P, 8, BANK], F32))

        scratch = nc.dram_tensor("weights_split", (UNITS, P, 2, 1024), F32, kind="Internal").ap()

        x_loaded = [sem(f"x_loaded{n}") for n in range(2)]
        consts_loaded = sem("consts_loaded")
        codes_loaded = [sem(f"codes_loaded{n}") for n in range(2)]
        t_ready = sem("t_ready")
        t_neg_ready = sem("t_neg_ready")
        lines_ready = sem("lines_ready")
        merged = sem("merged")
        summed = sem("summed")
        w_ready = sem("w_ready")
        w_turned = sem("w_turned")
        hi_ready = sem("hi_ready")
        lo_ready = sem("lo_ready")
        spilled = [sem(f"spilled{n}") for n in range(2)]
        reloaded = [sem(f"reloaded{n}") for n in range(2)]
        down_used = sem("down_used")
        gate_done = sem("gate_done")
        up_done = sem("up_done")
        silu_done = sem("silu_done")
        hid_done = sem("hid_done")
        hs_hi_ready = sem("hs_hi_ready")
        hs_ready = sem("hs_ready")
        x_updated = sem("x_updated")
        const_set = sem("const_set")
        maxima_set = sem("maxima_set")
        waits_passed = sem("waits_passed")
        norm_stats = sem("norm_stats")
        norm_moments = sem("norm_moments")
        rstd_step = sem("rstd_step")
        rstd_ready = sem("rstd_ready")
        xn_ready = sem("xn_ready")
        xn_turned = sem("xn_turned")
        xT_hi_ready = sem("xT_hi_ready")
        xT_ready = sem("xT_ready")
        stored = sem("stored")
        raw_loaded = [sem("wqkv_loaded"), sem("wo_loaded")]
        raw_hi = sem("raw_hi")
        raw_split = sem("raw_split")
        xs_used = sem("xs_used")
        qkv_taken = sem("qkv_taken")
        qk_biased = sem("qk_biased")
        k_rope = sem("k_rope")
        q_rope = sem("q_rope")
        pads_set = sem("pads_set")
        stack_hi = sem("stack_hi")
        q_stacked = sem("q_stacked")
        k_stacked = sem("k_stacked")
        v_staged = sem("v_staged")
        side_ready = sem("side_ready")
        side_taken = {"act": sem("side_taken_act"), "dve": sem("side_taken_dve")}
        row_max_step = sem("row_max_step")
        max_stacked = sem("max_stacked")
        scored = sem("scored")
        exp_done = sem("exp_done")
        diag_masked = sem("diag_masked")
        pv_done = sem("pv_done")
        ctxT_taken = sem("ctxT_taken")
        inverted = sem("inverted")
        ctx_turned = sem("ctx_turned")
        ctx_hi = sem("ctx_hi")
        ctx_lo = sem("ctx_lo")
        projected = sem("projected")
        bias_added = sem("bias_added")
        x_attended = sem("x_attended")

        PV_STEPS = [(half, kt) for half in range(2) for kt in range((half + 1) * HT)]
        NPV = len(PV_STEPS)
        DIAG = [kt * P >= half * HALF for half, kt in PV_STEPS]
        NDIAG = sum(DIAG)

        def first_col(half, kt):
            return max(0, kt * P - half * HALF)

        MAX_TILES = []
        for st in range(ST):
            for c in range(0, (st + 1) * P, BANK):
                width = min((st + 1) * P - c, BANK)
                for r in range(2):
                    heads = list(range(r, GH, 2))
                    MAX_TILES += [(st, c, width, heads)] if 2 * width <= BANK else [(st, c, width, [j]) for j in heads]
        NMAX = len(MAX_TILES)
        NMAX_LOW = len([tile for tile in MAX_TILES if tile[0] < HT])

        TURNS = [(operand, pair, half) for half in range(2) for operand in "kq" for pair in range(2)]
        TURNS += [("m", pair, half) for half in range(2) for pair in range(2)]

        SIDE_KINDS = ("turn", "max", "turn_ctx")
        SIDE_BANK, SIDE_BANKS, PV_BANK = 5, 3, 4

        def side_work():
            turns = [("turn", n, 1) for n in range(len(TURNS))]
            maxs = [("max", n, 1) for n in range(NMAX)]
            early = turns[0:4] + maxs[0:2] + turns[4:8] + maxs[2:NMAX_LOW] + [("stack_max", 0, 1)]
            late = maxs[NMAX_LOW:NMAX_LOW + 3] + turns[8:10] + maxs[NMAX_LOW + 3:]
            items = early + late
            work = [[] for _ in range(NPV)]
            steps = NPV - 1
            for n, item in enumerate(items):
                work[1 + n * steps // len(items)].append(item)
            return work, [("stack_max", 1, 1)], turns[10:12]

        def group_plan(before, this, following):
            work, stack_last, turn_last = side_work() if following else ([[]] * NPV, [], [])
            plan = [("stack", 0, 1)] if following else []
            for n in range(NPV):
                side = list(work[n])
                if before and n == 2:
                    side.append(("turn_ctx", 1, -1))
                if this and n == HT + 2:
                    side.append(("turn_ctx", 0, 0))
                a, b = -(-len(side) // 3), -(-2 * len(side) // 3)
                if this:
                    plan.append(("score", 2 * n, 0))
                plan += side[:a]
                if this:
                    plan.append(("score", 2 * n + 1, 0))
                plan += side[a:b]
                if n == NPV - 1:
                    plan += side[b:] + stack_last
                    side = side[:b]
                if this and n >= 1:
                    plan.append(("pv", n - 1, 0))
                if before and n == 0:
                    plan += [("pv", NPV - 1, -1), ("take_ctx", 1, -1)]
                if this and n == HT:
                    plan.append(("take_ctx", 0, 0))
                if following and n == 1:
                    plan.append(("stage_v", 0, 1))
                plan += side[b:]
            return plan + turn_last

        def side_engine(kind, n):
            return "act" if kind == "turn" and n % 2 == 0 else "dve"

        def sides_of(plan):
            return [side_engine(kind, n) for kind, n, _ in plan if kind in SIDE_KINDS]

        LEAD_PLAN, FIRST_PLAN = group_plan(False, False, True), group_plan(False, True, True)
        BODY_PLAN, LAST_PLAN = group_plan(True, True, True), group_plan(True, True, False)
        END_PLAN = [("pv", NPV - 1, -1), ("take_ctx", 1, -1), ("turn_ctx", 1, -1)]

        def leading(g):
            return isinstance(g, int) and g < 0

        def wait_apart(eng, signal, count):
            eng.wait_ge(signal, count)
            eng.sem_inc(waits_passed, 1)

        def sides_before(g, engine=None):
            def of(plan):
                return len([e for e in sides_of(plan) if engine in (None, e)])

            if isinstance(g, int) and g <= 0:
                return of(LEAD_PLAN) * (g + 1)
            before = of(LEAD_PLAN) + of(FIRST_PLAN)
            if isinstance(g, int) and g == GROUPS:
                return before + of(BODY_PLAN) * (g - 2) + of(LAST_PLAN)
            return before + of(BODY_PLAN) * (g - 1)

        def run_groups(eng, run_plan):
            run_plan(LEAD_PLAN, -1, 1)
            run_plan(FIRST_PLAN, 0, 0)
            with eng.Fori(0, GROUPS // 2 - 1) as i:
                for u in range(2):
                    run_plan(BODY_PLAN, 2 * i + 1 + u, 1 - u)
            run_plan(LAST_PLAN, GROUPS - 1, 1)
            run_plan(END_PLAN, GROUPS, 0)

        x_dram = x[0].rearrange("(t p) e -> p t e", p=P)
        out_dram = out[0].rearrange("(t p) e -> p t e", p=P)
        down_dram = down_q.rearrange("(c p) m -> p c m", p=P)

        CONSTS = 8

        def wait_unit_free(eng, call, n):
            if isinstance(n, int) and n >= MT + 2:
                eng.wait_ge(down_used, 2 * DU * call + n - MT - 1)
            elif isinstance(n, int) and n < 2 and call > 0:
                eng.wait_ge(down_used, 2 * DU * call + n - 1)
            else:
                eng.wait_ge(up_done, 2 * MT * call + 2 * n + 2)

        def reload_count(v):
            first = UNITS + (v - UNITS) % 2
            return (v - first) // 2 + 1

        def rope(eng, nat, biased, swapped, st, ready, steps):
            dst = nat[:, bass.ds(st, 1), :].rearrange("p a (h t d) -> p (a h) t d", t=2, d=D // 2)
            src = biased[:, :].rearrange("p (h t d) -> p h t d", t=2, d=D // 2)
            tmp = swapped[:, :].rearrange("p (h t d) -> p h t d", t=2, d=D // 2)
            cos, sin = (tab[:, bass.ds(st, 1), :].rearrange("p a (t d) -> p a t d", t=2)
                        .broadcast_to([P, HEADS, 2, D // 2]) for tab in (cos_t, sin_t))
            wait_apart(eng, *ready)
            eng.tensor_tensor(dst, src, cos, ALU.mult).then_inc(steps, 1)
            eng.tensor_tensor(tmp, src[:, :, ::-1, :], sin, ALU.mult).then_inc(steps, 1)
            wait_apart(eng, steps, 3 * st + 3)
            eng.tensor_tensor(dst, dst, tmp, ALU.add).then_inc(steps, 1)

        def take_turn(eng, n, u, bank):
            operand, pair, half = TURNS[n]
            dst = {"k": kT[u], "q": qT, "m": qTm[u]}[operand][:, pair, half * HALF:(half + 1) * HALF]
            if side_engine("turn", n) == "act":
                eng.activation(dst, ps[:, bank, :], ACT.Copy).then_inc(side_taken["act"], 1)
            else:
                eng.tensor_copy(dst, ps[:, bank, :]).then_inc(side_taken["dve"], 1)

        block = top.enter_context(nc.Block())

        @block.sync
        def _(sp):
            def load_gate_up(s, u, k):
                cv = codes[u][:, :].rearrange("p (a e) -> p a e", a=2)
                sp.dma_start(cv[:, 0:1, :], gate_q.rearrange("(t p) e -> p t e", p=P)[:, bass.ds(s, 1), :]
                             ).then_inc(codes_loaded[u], 16)
                sp.dma_start(cv[:, 1:2, :], up_q.rearrange("(t p) e -> p t e", p=P)[:, bass.ds(s, 1), :]
                             ).then_inc(codes_loaded[u], 16)

            def load_down(p, u):
                cv = codes[u][:, :].rearrange("p (c m) -> p c m", c=KT)
                for c in range(0, KT, 2):
                    sp.dma_start(cv[:, c:c + 2, :], down_dram[:, c:c + 2, bass.ds(2 * P * p, 2 * P)]
                                 ).then_inc(codes_loaded[u], 16)

            def spill(s, u):
                sp.wait_ge(lo_ready, s + 2)
                sp.dma_start(scratch[bass.ds(s, 1)].rearrange("a p h n -> (a p) h n"), wT[u][:, :, :].bitcast(F32)
                             ).then_inc(spilled[u], 16)

            def reload(s, call, n, u):
                wait_unit_free(sp, call, n)
                sp.dma_start(wT[u][:, :, :].bitcast(F32), scratch[bass.ds(s, 1)].rearrange("a p h n -> (a p) h n")
                             ).then_inc(reloaded[u], 16)

            for n in range(2):
                sp.sem_inc(spilled[n], 16)
            sp.dma_start(xres[:, 0:HT, :], x_dram[:, 0:HT, :]).then_inc(x_loaded[0], 16)
            load_gate_up(0, 0, 1)
            sp.dma_start(ident[:, :], identity).then_inc(consts_loaded, 16)
            sp.dma_start(absmax_gu[:, 0], gate_absmax.rearrange("(t p b) -> p t b", p=P, t=MT)).then_inc(consts_loaded, 16)
            sp.dma_start(absmax_gu[:, 1], up_absmax.rearrange("(t p b) -> p t b", p=P, t=MT)).then_inc(consts_loaded, 16)
            sp.dma_start(absmax_d[:, :, :], down_absmax.rearrange("(c p b) -> p c b", p=P, c=KT)).then_inc(consts_loaded, 16)
            sp.dma_start(xres[:, HT:ST, :], x_dram[:, HT:ST, :]).then_inc(x_loaded[1], 16)
            sp.dma_start(cos_t[:, :, :], rope_cos.rearrange("(t p) d -> p t d", p=P)).then_inc(consts_loaded, 16)
            sp.dma_start(sin_t[:, :, :], rope_sin.rearrange("(t p) d -> p t d", p=P)).then_inc(consts_loaded, 16)
            sp.dma_start(qkv_bias[:, :], qkv_b.rearrange("(a n) -> a n", a=1).broadcast_to([P, 3 * E])).then_inc(consts_loaded, 16)
            sp.dma_start(out_bias[:, :], out_b.rearrange("(a n) -> a n", a=1).broadcast_to([P, E])).then_inc(consts_loaded, 16)
            load_gate_up(1, 1, 1)
            with sp.Fori(0, MT // 2 - 1) as i:
                for u in range(2):
                    s = 2 * i + u
                    sp.wait_ge(t_ready, s + 1)
                    load_gate_up(s + 2, u, i + 2)
                    spill(s, u)
            for s in range(MT - 2, UNITS):
                if s + 2 < UNITS:
                    sp.wait_ge(t_ready, s + 1)
                    load_down(s + 2 - MT, s % 2)
                spill(s, s % 2)
            for n in range(2):
                sp.wait_ge(spilled[n], 16 + 16 * ((UNITS + 1 - n) // 2))
            sp.wait_ge(summed, UNITS + 1)
            sp.dma_start(raw_w[:, :, :], qkv_w.rearrange("(c p) n -> p c n", p=P)).then_inc(raw_loaded[0], 16)
            for p in range(DU):
                reload(MT + p, 0, UNITS + p, (UNITS + p) % 2)
            sp.wait_ge(raw_split, KT)
            sp.dma_start(raw_w[:, :, 0:E], out_w.rearrange("(c p) n -> p c n", p=P)).then_inc(raw_loaded[1], 16)

            sp.wait_ge(projected, ST + CREDIT)
            for n in range(2):
                reload(n, 1, n, n)
            with sp.Fori(0, MT // 2 - 1) as i:
                for u in range(2):
                    reload(2 * i + u + 2, 1, 2 * i + u + 2, u)
            for p in range(DU):
                reload(MT + p, 1, MT + p, (MT + p) % 2)
            for p in range(DU):
                reload(MT + p, 1, UNITS + p, (UNITS + p) % 2)

            sp.wait_ge(x_updated, 2 * ST)
            sp.dma_start(out_dram, xres[:, :, :]).then_inc(stored, 16)
            sp.wait_ge(stored, 16)

        @block.gpsimd
        def _(pool):
            def shift_codes(s, u, k):
                wait_apart(pool, codes_loaded[u], 32 * k)
                pool.tensor_scalar(t_code[:, u, :], codes[u][:, :], 1.0, -7.0, ALU.mult, ALU.add).then_inc(t_ready, 1)

            def scale_unit(s, absmax, shape):
                pool.wait_ge(merged, MERGES * (s + 2))
                pool.wait_ge(w_turned, s + 1)
                pool.tensor_tensor(w_scaled[:, :], lines[:, LINE_SLOT["n01"], :], lines[:, LINE_SLOT["p89"], :],
                                   ALU.add).then_inc(summed, 1)
                pool.wait_ge(summed, s + 2)
                wv = w_scaled[:, :].rearrange("p (a b n) -> p a b n", a=shape[0], b=shape[1])
                pool.tensor_tensor(wv, wv, absmax.unsqueeze(3).broadcast_to([P, *shape, NF4_BLOCK]),
                                   ALU.mult).then_inc(w_ready, 1)

            def scale_gate_up(s):
                scale_unit(s, absmax_gu[:, :, bass.ds(s, 1), :].rearrange("p a t b -> p a (t b)"), (2, E // NF4_BLOCK))

            def scale_down(s):
                scale_unit(s, absmax_d[:, :, bass.ds(4 * (s - MT), 4)], (KT, 2 * P // NF4_BLOCK))

            def inverse_deviation(half, first):
                pool.wait_ge(norm_moments, first + ST // 2 * (half + 1))
                a, b = half * HT, (half + 1) * HT
                base = rstd_steps[0]

                def step(ins):
                    rstd_steps[0] += 1
                    ins.then_inc(rstd_step, 1)
                    pool.wait_ge(rstd_step, rstd_steps[0])

                ve, r, rr, c = (rstd_tmp[:, n, :] for n in range(4))
                step(pool.tensor_scalar(ve, moments[:, a:b, 1], 1.0, EPS, ALU.mult, ALU.add))
                step(pool.tensor_tensor(r, ve, minus_half[:, :], ALU.pow))
                step(pool.tensor_tensor(rr, r, r, ALU.mult))
                step(pool.tensor_tensor(c, rr, ve, ALU.mult))
                step(pool.tensor_scalar(rr, c, -0.5, 1.5, ALU.mult, ALU.add))
                pool.tensor_tensor(rstd[:, a:b], r, rr, ALU.mult).then_inc(rstd_ready, 1)

            rstd_steps = [0]
            pool.memset(minus_half[:, :], -0.5).then_inc(const_set, 1)
            pool.memset(causal_mask[:, :], 0.0).then_inc(const_set, 1)
            pool.wait_ge(const_set, 2)
            pool.affine_select(out=causal_mask[:, :], in_=causal_mask[:, :], compare_op=ALU.is_ge,
                               fill=MASKED, base=0, pattern=[[-1, P]], channel_multiplier=1).then_inc(const_set, 1)
            pool.sem_inc(summed, 1)
            pool.wait_ge(const_set, 3)
            shift_codes(0, 0, 1)
            shift_codes(1, 1, 1)
            inverse_deviation(0, 0)
            inverse_deviation(1, 0)
            pool.wait_ge(consts_loaded, 16 * CONSTS)
            pool.tensor_copy(ident_bf16[:, :], ident[:, :]).then_inc(const_set, 1)
            with pool.Fori(0, MT // 2 - 1) as i:
                for u in range(2):
                    scale_gate_up(2 * i + u)
                    shift_codes(2 * i + u + 2, u, i + 2)
            for s in range(MT - 2, UNITS):
                (scale_gate_up if s < MT else scale_down)(s)
                if s + 2 < UNITS:
                    shift_codes(s + 2, s % 2, (s + 2) // 2 + 1)

            for half in range(2):
                inverse_deviation(half, ST)

            pool.sem_inc(q_rope, 1)
            with pool.Fori(0, ST) as st:
                rope(pool, q_nat, q_biased, q_swapped, st, (qk_biased, 2 * st + 1), q_rope)

            pool.wait_ge(xs_used, ST + CREDIT)
            pool.wait_ge(k_rope, 3 * ST + 1)
            pool.wait_ge(q_rope, 3 * ST + 1)
            pool.wait_ge(raw_split, KT + 1)
            pool.memset(stack_k[:, :, :, KA:KB], 1.0).then_inc(pads_set, 1)
            pool.memset(stack_k[:, :, :, KB:SLOT], 0.0).then_inc(pads_set, 1)
            pool.memset(stack_q[:, :, :, KA:SLOT], 0.0).then_inc(pads_set, 1)
            for n in range(2):
                pool.memset(v_ext[n][:, :, :, D:D + 1], 1.0).then_inc(pads_set, 1)
                pool.memset(v_ext[n][:, :, :, D + 1:32], 0.0).then_inc(pads_set, 1)

            def attend(plan, g, u):
                for kind, n, rel in plan:
                    if kind == "stack":
                        qg = q_nat[:, :, bass.ds((g + 1) * GW, GW)].rearrange("p t (j d) -> p t j d", j=GH)
                        wait_apart(pool, stack_hi, 2 * (g + 1) + 1)
                        pool.tensor_tensor(stack_q[:, :, :, D:2 * D], qg, stack_q[:, :, :, 0:D], ALU.subtract
                                           ).then_inc(q_stacked, 1)
                        pool.tensor_scalar(stack_q[:, :, :, 2 * D:3 * D], stack_q[:, :, :, 0:D], 1.0, 0.0, ALU.mult,
                                           ALU.add).then_inc(q_stacked, 1)
                    if kind == "score" and DIAG[n // 2]:
                        half, kt = PV_STEPS[n // 2]
                        c = first_col(half, kt)
                        tile = probs[n // 2 % 2][n % 2][:, :, c:c + P]
                        wait_apart(pool, exp_done, 2 * NPV * g + n + 1 + CREDIT)
                        pool.affine_select(out=tile, in_=tile, compare_op=ALU.is_ge, fill=0.0, base=0,
                                           pattern=[[0, 2], [1, P]], channel_multiplier=-1).then_inc(diag_masked, 1)

            run_groups(pool, attend)

            pool.wait_ge(consts_loaded, 16 * CONSTS)
            for half in range(2):
                inverse_deviation(half, 2 * ST)

        @block.scalar
        def _(act):
            def line(name, s, u, src):
                a, b = NF4_LINES[name]
                act.activation(lines[:, LINE_SLOT[name], :], src[:, u, :], ACT.Copy, bias=b, scale=a).then_inc(lines_ready, 1)

            def lines_first(s, u):
                act.wait_ge(t_ready, s + 1)
                act.wait_ge(merged, MERGES * s + 1)
                line("p1011", s, u, t_code)
                act.wait_ge(merged, MERGES * s + 3)
                line("p1213", s, u, t_code)
                act.wait_ge(t_neg_ready, s + 1)
                line("n23", s, u, t_neg)
                act.wait_ge(merged, MERGES * s + 5)
                line("n45", s, u, t_neg)

            def lines_last(s, u):
                act.wait_ge(merged, MERGES * s + 6)
                line("p1415", s, u, t_code)
                act.wait_ge(summed, s + 1)
                line("n01", s, u, t_neg)
                line("p89", s, u, t_code)

            def split_hi(s, u, k):
                act.wait_ge(w_turned, s + 2)
                wait_unit_free(act, 0, s)
                act.wait_ge(spilled[u], 16 * k)
                act.activation(wT[u][:, 0, :].rearrange("p (a n) -> p a n", a=2), ps[:, 4:6, :], ACT.Copy
                               ).then_inc(hi_ready, 1)

            def silu(call, mt, half):
                n = 2 * MT * call + 2 * mt + half
                act.wait_ge(gate_done, n + 1)
                act.wait_ge(hid_done, n + 1)
                act.activation(silu_g[:, half, :], ps[:, 2 * half, :], ACT.Silu).then_inc(silu_done, 1)

            def hs_hi(call, n, u, half, p):
                wait_unit_free(act, call, n)
                act.activation(hs[u][:, 0, :, :], hid[:, bass.ds(2 * p, 2), half * HALF:(half + 1) * HALF], ACT.Copy
                               ).then_inc(hs_hi_ready, 1)

            def norm_hi(n, st):
                act.wait_ge(xn_turned, n + 1)
                act.activation(xT_hi[:, :, st * P:(st + 1) * P], ps[:, 6 + n % 2, :].rearrange("p (k s) -> p k s", k=KT),
                               ACT.Copy).then_inc(xT_hi_ready, 1)

            act.sem_inc(exp_done, CREDIT)
            act.sem_inc(ctxT_taken, 1)
            act.preload_act_table(ACT.Silu)
            lines_first(0, 0)
            lines_last(0, 0)
            for st in range(HT):
                norm_hi(st, st)
            lines_first(1, 1)
            lines_last(1, 1)
            for st in range(HT, ST):
                norm_hi(st, st)
            split_hi(0, 0, 1)
            lines_first(2, 0)
            lines_last(2, 0)
            with act.Fori(0, MT // 2 - 1) as i:
                for w in range(2):
                    s, u = 2 * i + 1 + w, (1 + w) % 2
                    split_hi(s, u, i + 1 + w)
                    lines_first(s + 2, u)
                    silu(0, s - 1, 0)
                    lines_last(s + 2, u)
                    silu(0, s - 1, 1)
            for s in range(MT - 1, UNITS):
                u = s % 2
                split_hi(s, u, s // 2 + 1)
                if s + 2 < UNITS:
                    lines_first(s + 2, u)
                if s <= MT:
                    silu(0, s - 1, 0)
                if s + 2 < UNITS:
                    lines_last(s + 2, u)
                if s <= MT:
                    silu(0, s - 1, 1)
                if s == MT:
                    act.wait_ge(hid_done, 2 * MT + CREDIT)
                if s >= MT:
                    hs_hi(0, s, u, 0, s - MT)
            for p in range(DU):
                v = UNITS + p
                hs_hi(0, v, v % 2, 1, p)
                if 2 <= p < 2 + KT:
                    c = p - 2
                    act.wait_ge(raw_loaded[0], 16)
                    act.activation(wqkv[0][:, c, :], raw_w[:, c, :], ACT.Copy).then_inc(raw_hi, 1)

            with act.Fori(0, ST // 2) as i:
                for u in range(2):
                    st = 2 * i + u
                    act.wait_ge(xn_turned, ST + st + 1)
                    act.wait_ge(xs_used, st + 1)
                    act.activation(xs[0][:, u, :, :], ps[:, 6 + u, :].rearrange("p (k s) -> p k s", k=KT), ACT.Copy
                                   ).then_inc(xT_hi_ready, 1)
            act.wait_ge(raw_loaded[1], 16)
            act.activation(wo[0][:, :, :], raw_w[:, :, 0:E], ACT.Copy).then_inc(raw_hi, 1)

            act.preload_act_table(ACT.Exp)
            act.wait_ge(pads_set, 3)

            def attend(plan, g, u):
                side = 0
                for kind, n, rel in plan:
                    if kind == "stack":
                        if not leading(g):
                            act.wait_ge(side_ready, sides_before(g))
                        cols = bass.ds((g + 1) * GW, GW)
                        for nat, stack in ((q_nat, stack_q), (k_nat, stack_k)):
                            act.activation(stack[:, :, :, 0:D].bitcast(F32R),
                                           nat[:, :, cols].rearrange("p t (j d) -> p t j d", j=GH), ACT.Copy
                                           ).then_inc(stack_hi, 1)
                    if kind == "score":
                        half, kt = PV_STEPS[n // 2]
                        c = first_col(half, kt)
                        act.wait_ge(scored, 2 * NPV * g + n + 1)
                        act.wait_ge(pv_done, NPV * g + n // 2 + 1)
                        act.activation(probs[n // 2 % 2][n % 2][:, :, c:HALF], ps[:, 2 * (n % 2):2 * (n % 2) + 2, c:HALF],
                                       ACT.Exp, scale=float(D) ** -0.5).then_inc(exp_done, 1)
                    if kind == "take_ctx":
                        act.wait_ge(pv_done, NPV * (g + rel) + CREDIT + (NPV if n else HT))
                        if not isinstance(g, int) or 2 * (g + rel) + n > 0:
                            act.wait_ge(inverted, 2 * (g + rel) + n)
                        act.activation(ctxT[:, :], ps[:, PV_BANK, :], ACT.Copy).then_inc(ctxT_taken, 1)
                    if kind in SIDE_KINDS:
                        if side_engine(kind, n) == "act":
                            act.wait_ge(side_ready, sides_before(g) + side + 1)
                            take_turn(nc.scalar, n, 1 - u, SIDE_BANK + side % SIDE_BANKS)
                        side += 1

            run_groups(act, attend)

            with act.Fori(0, ST // 2) as i:
                for u in range(2):
                    st = 2 * i + u
                    act.wait_ge(ctx_turned, st + 1)
                    act.wait_ge(projected, st + 1)
                    act.activation(xs[0][:, u, :, :], ps[:, 2 + u, :].rearrange("p (k s) -> p k s", k=KT), ACT.Copy
                                   ).then_inc(ctx_hi, 1)

            act.preload_act_table(ACT.Silu)
            for st in range(ST):
                norm_hi(2 * ST + st, st)
            with act.Fori(0, MT) as mt:
                for half in range(2):
                    silu(1, mt, half)
            act.wait_ge(hid_done, 4 * MT + CREDIT)
            for half in range(2):
                for p in range(DU):
                    n = MT + DU * half + p
                    hs_hi(1, n, n % 2, half, p)

        @block.vector
        def _(dve):
            def slot(name):
                return lines[:, LINE_SLOT[name], :]

            def clamp_codes(s, u):
                dve.wait_ge(t_ready, s + 1)
                dve.tensor_scalar(t_neg[:, u, :], t_code[:, u, :], 0.0, None, ALU.min).then_inc(t_neg_ready, 1)

            def own(s, k):
                dve.wait_ge(merged, MERGES * (s + 1) + k)

            def merge_first(s):
                dve.wait_ge(lines_ready, LINES * s + 2)
                dve.tensor_tensor(slot("p1213"), slot("p1011"), slot("p1213"), ALU.max).then_inc(merged, 1)
                dve.wait_ge(lines_ready, LINES * s + 4)
                dve.tensor_tensor(slot("n45"), slot("n23"), slot("n45"), ALU.min).then_inc(merged, 1)

            def merge_last(s, u):
                dve.wait_ge(lines_ready, LINES * s + 5)
                own(s, 1)
                dve.tensor_tensor(slot("p1415"), slot("p1213"), slot("p1415"), ALU.max).then_inc(merged, 1)
                dve.wait_ge(lines_ready, LINES * s + 6)
                own(s, 2)
                dve.tensor_tensor(slot("n45"), slot("n01"), slot("n45"), ALU.min).then_inc(merged, 1)
                own(s, 4)
                dve.scalar_tensor_tensor(slot("n01"), t_neg[:, u, :], NF4_SLOPE_67, slot("n45"), ALU.mult, ALU.min
                                         ).then_inc(merged, 1)
                dve.wait_ge(lines_ready, LINES * s + 7)
                own(s, 3)
                dve.scalar_tensor_tensor(slot("p89"), slot("p1415"), 0.0, slot("p89"), ALU.max, ALU.max
                                         ).then_inc(merged, 1)

            def split_lo(s, u):
                dve.wait_ge(hi_ready, s + 1)
                dve.tensor_tensor(wT[u][:, 1, :].rearrange("p (a n) -> p a n", a=2), ps[:, 4:6, :],
                                  wT[u][:, 0, :].rearrange("p (a n) -> p a n", a=2).bitcast(F32), ALU.subtract
                                  ).then_inc(lo_ready, 1)

            def hidden(call, mt, half):
                n = 2 * MT * call + 2 * mt + half
                dve.wait_ge(silu_done, n + 1)
                dve.wait_ge(up_done, n + 5)
                dve.tensor_tensor(hid[:, bass.ds(mt, 1), half * HALF:(half + 1) * HALF].rearrange("p a n -> p (a n)"),
                                  silu_g[:, half, :], ps[:, 2 * half + 1, :], ALU.mult).then_inc(hid_done, 1)

            def hs_lo(k, u, half, p):
                dve.wait_ge(hs_hi_ready, k)
                dve.tensor_tensor(hs[u][:, 1, :, :], hid[:, bass.ds(2 * p, 2), half * HALF:(half + 1) * HALF],
                                  hs[u][:, 0, :, :].bitcast(F32), ALU.subtract).then_inc(hs_ready, 1)

            def add_down(n, half):
                dve.wait_ge(down_used, DU * (n + 1))
                for t in range(HT):
                    st = half * HT + t
                    dve.scalar_tensor_tensor(xres[:, st, :], ps[:, 4 * half + t, :], 0.5, xres[:, st, :],
                                             ALU.mult, ALU.add).then_inc(x_updated, 1)

            def norm_statistics(n0, half):
                for st in range(half * HT, (half + 1) * HT):
                    dve.bn_stats(stats[:, st, :], xres[:, st, :]).then_inc(norm_stats, 1)
                for st in range(half * HT, (half + 1) * HT):
                    dve.wait_ge(norm_stats, n0 + st + 1)
                    dve.bn_aggr(moments[:, st, :], stats[:, st, :]).then_inc(norm_moments, 1)

            def moments_of(st):
                return moments[:, bass.ds(st, 1), 0:1].rearrange("p a b -> p (a b)")

            def rstd_of(st):
                return rstd[:, bass.ds(st, 1)]

            def norm_half(n0, half):
                tiles = range(half * HT, (half + 1) * HT)
                norm_statistics(n0, half)
                dve.wait_ge(rstd_ready, n0 // HT + half + 1)

                def normalize(st):
                    dve.tensor_scalar(xn[:, st % 2, :], xres[:, st, :], moments[:, st, 0:1], rstd[:, st:st + 1],
                                      ALU.subtract, ALU.mult).then_inc(xn_ready, 1)

                def norm_lo(st):
                    dve.wait_ge(xT_hi_ready, n0 + st + 1)
                    dve.tensor_tensor(xT_lo[:, :, st * P:(st + 1) * P],
                                      ps[:, 6 + st % 2, :].rearrange("p (k s) -> p k s", k=KT),
                                      xT_hi[:, :, st * P:(st + 1) * P].bitcast(F32), ALU.subtract).then_inc(xT_ready, 1)

                normalize(tiles[0])
                for st in tiles:
                    if st + 1 in tiles:
                        normalize(st + 1)
                    norm_lo(st)

            dve.sem_inc(merged, MERGES)
            dve.sem_inc(lo_ready, 1)
            dve.sem_inc(hid_done, CREDIT)
            dve.sem_inc(qkv_taken, CREDIT)
            dve.sem_inc(k_rope, 1)
            clamp_codes(0, 0)
            clamp_codes(1, 1)
            dve.wait_ge(x_loaded[0], 16)
            norm_half(0, 0)
            merge_first(0)
            merge_last(0, 0)
            dve.wait_ge(x_loaded[1], 16)
            norm_half(0, 1)
            merge_first(1)
            merge_last(1, 1)
            split_lo(0, 0)
            clamp_codes(2, 0)
            merge_first(2)
            merge_last(2, 0)
            with dve.Fori(0, MT // 2 - 1) as i:
                for w in range(2):
                    s, u = 2 * i + 1 + w, (1 + w) % 2
                    split_lo(s, u)
                    clamp_codes(s + 2, u)
                    merge_first(s + 2)
                    hidden(0, s - 1, 0)
                    merge_last(s + 2, u)
                    hidden(0, s - 1, 1)
            for s in range(MT - 1, UNITS):
                u = s % 2
                split_lo(s, u)
                if s + 2 < UNITS:
                    clamp_codes(s + 2, u)
                    merge_first(s + 2)
                if s <= MT:
                    hidden(0, s - 1, 0)
                if s + 2 < UNITS:
                    merge_last(s + 2, u)
                if s <= MT:
                    hidden(0, s - 1, 1)
                if s >= MT:
                    hs_lo(s - MT + 1, u, 0, s - MT)
            add_down(0, 0)
            for p in range(DU):
                v = UNITS + p
                hs_lo(DU + p + 1, v % 2, 1, p)
                if 2 <= p < 2 + KT:
                    c = p - 2
                    dve.wait_ge(raw_hi, c + 1)
                    dve.tensor_tensor(wqkv[1][:, c, :], raw_w[:, c, :], wqkv[0][:, c, :].bitcast(F32), ALU.subtract
                                      ).then_inc(raw_split, 1)
            add_down(1, 1)

            for half in range(2):
                norm_statistics(ST, half)
            dve.wait_ge(rstd_ready, 4)
            dve.wait_ge(consts_loaded, 16 * CONSTS)

            def normalize_tile(st, u):
                dve.tensor_scalar(xn[:, u, :], xres[:, bass.ds(st, 1), :].rearrange("p a e -> p (a e)"),
                                  moments_of(st), rstd_of(st), ALU.subtract, ALU.mult).then_inc(xn_ready, 1)

            def tile_lo(st, u):
                dve.wait_ge(xT_hi_ready, ST + st + 1)
                dve.tensor_tensor(xs[1][:, u, :, :], ps[:, 6 + u, :].rearrange("p (k s) -> p k s", k=KT),
                                  xs[0][:, u, :, :].bitcast(F32), ALU.subtract).then_inc(xT_ready, 1)

            def take_qkv(st, u):
                dve.wait_ge(xs_used, st + 1 + CREDIT)
                dve.wait_ge(q_rope, 3 * st + 1)
                dve.tensor_tensor(q_biased[:, :], ps[:, 3 * u, :], qkv_bias[:, 0:E], ALU.add).then_inc(qk_biased, 1)
                dve.tensor_tensor(k_biased[:, :], ps[:, 3 * u + 1, :], qkv_bias[:, E:2 * E], ALU.add).then_inc(qk_biased, 1)
                dve.tensor_tensor(v_nat[:, bass.ds(st, 1), :].rearrange("p a e -> p (a e)"), ps[:, 3 * u + 2, :],
                                  qkv_bias[:, 2 * E:3 * E], ALU.add).then_inc(qkv_taken, 1)
                rope(dve, k_nat, k_biased, k_swapped, st, (qk_biased, 2 * st + 2), k_rope)

            normalize_tile(0, 0)
            normalize_tile(1, 1)
            tile_lo(0, 0)
            with dve.Fori(0, ST // 2 - 1) as i:
                for u in range(2):
                    st = 2 * i + u
                    normalize_tile(st + 2, u)
                    tile_lo(st + 1, 1 - u)
                    take_qkv(st, u)
            tile_lo(ST - 1, 1)
            take_qkv(ST - 2, 0)
            take_qkv(ST - 1, 1)
            dve.wait_ge(raw_hi, KT + 1)
            dve.tensor_tensor(wo[1][:, :, :], raw_w[:, :, 0:E], wo[0][:, :, :].bitcast(F32), ALU.subtract
                              ).then_inc(raw_split, 1)

            dve.wait_ge(xs_used, ST + CREDIT)
            dve.wait_ge(pads_set, 7)
            dve.memset(maxima[:, :, :, :], -3.0e38).then_inc(maxima_set, 1)
            dve.wait_ge(maxima_set, 1)

            def attend(plan, g, u):
                side = 0
                for kind, n, rel in plan:
                    bank = SIDE_BANK + side % SIDE_BANKS
                    if kind == "stack":
                        kg = k_nat[:, :, bass.ds((g + 1) * GW, GW)].rearrange("p t (j d) -> p t j d", j=GH)
                        dve.wait_ge(stack_hi, 2 * (g + 1) + 2)
                        dve.tensor_copy(stack_k[:, :, :, D:2 * D], stack_k[:, :, :, 0:D]).then_inc(k_stacked, 1)
                        dve.tensor_tensor(stack_k[:, :, :, 2 * D:3 * D], kg, stack_k[:, :, :, 0:D], ALU.subtract
                                          ).then_inc(k_stacked, 1)
                    if kind == "stage_v":
                        if not leading(g):
                            dve.wait_ge(pv_done, NPV * g + CREDIT)
                        dve.tensor_copy(v_ext[1 - u][:, :, :, 0:D],
                                        v_nat[:, :, bass.ds((g + 1) * GW, GW)].rearrange("p t (j d) -> p t j d", j=GH)
                                        ).then_inc(v_staged, 1)
                    if kind == "turn" and side_engine(kind, n) == "dve":
                        dve.wait_ge(side_ready, sides_before(g) + side + 1)
                        take_turn(nc.vector, n, 1 - u, bank)
                    if kind == "max":
                        st, c, width, heads = MAX_TILES[n]
                        dve.wait_ge(side_ready, sides_before(g) + side + 1)
                        dve.tensor_reduce(maxima[:, c // BANK, st, heads[0]:heads[-1] + 1:2],
                                          ps[:, bank, 0:len(heads) * width].rearrange("p (j n) -> p j n", n=width),
                                          AX.X, ALU.max).then_inc(side_taken["dve"], 1)
                    if kind == "stack_max":
                        tiles = slice(n * HT, (n + 1) * HT)
                        dve.wait_ge(side_taken["dve"], sides_before(g, "dve") + sides_of(plan)[:side].count("dve"))
                        dve.tensor_tensor(row_max[:, tiles, :], maxima[:, 0, tiles, :], maxima[:, 1, tiles, :], ALU.max
                                          ).then_inc(row_max_step, 1)
                        dve.wait_ge(row_max_step, 2 * (g + 1) + n + 1)
                        dve.tensor_scalar(stack_q[:, tiles, :, KA].bitcast(F32R), row_max[:, tiles, :], -1.0, None,
                                          ALU.mult).then_inc(max_stacked, 1)
                        dve.wait_ge(max_stacked, 4 * (g + 1) + 2 * n + 1)
                        dve.scalar_tensor_tensor(stack_q[:, tiles, :, KA + 1], row_max[:, tiles, :], -1.0,
                                                 stack_q[:, tiles, :, KA], ALU.mult, ALU.subtract
                                                 ).then_inc(max_stacked, 1)
                    if kind == "turn_ctx":
                        gc = g + rel
                        dve.wait_ge(side_ready, sides_before(g) + side + 1)
                        tile = ps[:, bank, :].rearrange("p (t j d) -> p t j d", t=HT, j=GH)
                        dve.reciprocal(inv_den[:, n, :, :], tile[:, :, :, D]).then_inc(inverted, 1)
                        dve.wait_ge(inverted, 2 * gc + n + 1)
                        dve.tensor_tensor(ctx_nat[:, n * HT:(n + 1) * HT, bass.ds(gc * GW, GW)]
                                          .rearrange("p t (j d) -> p t j d", j=GH), tile[:, :, :, 0:D],
                                          inv_den[:, n, :, :].unsqueeze(3).broadcast_to([P, HT, GH, D]), ALU.mult
                                          ).then_inc(side_taken["dve"], 1)
                    if kind in SIDE_KINDS:
                        side += 1

            run_groups(dve, attend)

            dve.sem_inc(ctx_lo, CREDIT)
            dve.sem_inc(x_attended, CREDIT)

            def ctx_low(st, u):
                dve.wait_ge(ctx_hi, st + 1)
                dve.tensor_tensor(xs[1][:, u, :, :], ps[:, 2 + u, :].rearrange("p (k s) -> p k s", k=KT),
                                  xs[0][:, u, :, :].bitcast(F32), ALU.subtract).then_inc(ctx_lo, 1)

            def add_attended(st, u):
                xt = xres[:, bass.ds(st, 1), :].rearrange("p a e -> p (a e)")
                dve.tensor_tensor(xt, xt, out_bias[:, :], ALU.add).then_inc(bias_added, 1)
                dve.wait_ge(bias_added, st + 1)
                dve.wait_ge(projected, st + 1 + CREDIT)
                dve.tensor_tensor(xt, xt, ps[:, u, :], ALU.add).then_inc(x_attended, 1)

            with dve.Fori(0, ST // 2) as i:
                for u in range(2):
                    ctx_low(2 * i + u, u)
                    add_attended(2 * i + u, u)

            dve.wait_ge(x_attended, ST + CREDIT)
            norm_half(2 * ST, 0)
            norm_half(2 * ST, 1)
            with dve.Fori(0, MT) as mt:
                for half in range(2):
                    hidden(1, mt, half)
            for half in range(2):
                for p in range(DU):
                    n = MT + DU * half + p
                    hs_lo(DU * (2 + half) + p + 1, n % 2, half, p)
                add_down(2 + half, half)

        @block.tensor
        def _(pe):
            def turn(s, src):
                pe.wait_ge(w_ready, s + 1)
                pe.wait_ge(lo_ready, s + 1)
                for b in range(8):
                    ins = pe.transpose(ps[:, 4 + b // 4, (b % 4) * P:(b % 4 + 1) * P], src(b), ident[:, :])
                ins.then_inc(w_turned, 1)

            def turn_gate_up(s):
                turn(s, lambda b: w_scaled[:, b * P:(b + 1) * P])

            def turn_down(s):
                wv = w_scaled[:, :].rearrange("p (c m) -> p c m", c=KT)
                turn(s, lambda b: wv[:, b % 4, (b // 4) * P:(b // 4 + 1) * P])

            def weights_ready(v, u, k):
                if k is None:
                    pe.wait_ge(lo_ready, v + 2)
                else:
                    pe.wait_ge(reloaded[u], 16 * k)

            def gate_up(call, mt, v, u, k=None):
                weights_ready(v, u, k)
                for half in range(2):
                    cols = slice(half * HALF, (half + 1) * HALF)
                    pe.wait_ge(hid_done, 2 * MT * call + 2 * mt + half + 1)
                    for g, done in ((0, gate_done), (1, up_done)):
                        bank = ps[:, 2 * half + g, :]
                        for kt in range(KT):
                            w = [wT[u][:, part, (4 * g + kt) * P:(4 * g + kt + 1) * P] for part in range(2)]
                            pe.matmul(bank, w[0], xT_hi[:, kt, cols], start=kt == 0, stop=False)
                            pe.matmul(bank, w[1], xT_hi[:, kt, cols], start=False, stop=False)
                            ins = pe.matmul(bank, w[0], xT_lo[:, kt, cols], start=False, stop=kt == KT - 1)
                        ins.then_inc(done, 1)

            def down(half, v, u, h, k, first, last):
                weights_ready(v, u, k)
                pe.wait_ge(hs_ready, h)
                for j in range(2):
                    for t in range(HT):
                        a = [hs[u][:, part, j, t * P:(t + 1) * P] for part in range(2)]
                        w = [wT[u][:, part, j * E:(j + 1) * E] for part in range(2)]
                        bank = ps[:, 4 * half + t, :]
                        pe.matmul(bank, a[0], w[0], start=first and j == 0, stop=False)
                        pe.matmul(bank, a[1], w[0], start=False, stop=False)
                        ins = pe.matmul(bank, a[0], w[1], start=False, stop=last and j == 1)
                ins.then_inc(down_used, 1)

            def norm_turn(n):
                pe.wait_ge(xn_ready, n + 1)
                if n >= 2:
                    pe.wait_ge(xT_ready, n - 1)
                for k in range(KT):
                    ins = pe.transpose(ps[:, 6 + n % 2, k * P:(k + 1) * P], xn[:, n % 2, k * P:(k + 1) * P], ident[:, :])
                ins.then_inc(xn_turned, 1)

            pe.sem_inc(w_turned, 1)
            pe.sem_inc(up_done, 4)
            pe.wait_ge(consts_loaded, 16 * CONSTS)
            for st in range(ST):
                norm_turn(st)
            turn_gate_up(0)
            pe.wait_ge(xT_ready, ST)
            with pe.Fori(0, MT // 2 - 1) as i:
                for w in range(2):
                    s, u = 2 * i + 1 + w, (1 + w) % 2
                    turn_gate_up(s)
                    gate_up(0, s - 1, s - 1, 1 - u)
            for s in range(MT - 1, UNITS):
                (turn_gate_up if s < MT else turn_down)(s)
                if s <= MT:
                    gate_up(0, s - 1, s - 1, (s - 1) % 2)
                else:
                    if s == MT + 1:
                        pe.wait_ge(hid_done, 2 * MT + CREDIT)
                    down(0, s - 1, (s - 1) % 2, s - MT, None, s == MT + 1, False)
            down(0, UNITS - 1, (UNITS - 1) % 2, DU, None, False, True)
            for p in range(DU):
                v = UNITS + p
                down(1, v, v % 2, DU + p + 1, reload_count(v), p == 0, p == DU - 1)

            pe.sem_inc(xs_used, CREDIT)
            pe.sem_inc(pv_done, CREDIT)

            def project(u, w, cols, banks, done):
                for b in range(cols // BANK):
                    c = slice(b * BANK, (b + 1) * BANK)
                    for kt in range(KT):
                        pe.matmul(ps[:, banks + b, :], xs[0][:, u, kt, :], w[0][:, kt, c], start=kt == 0, stop=False)
                        pe.matmul(ps[:, banks + b, :], xs[1][:, u, kt, :], w[0][:, kt, c], start=False, stop=False)
                        ins = pe.matmul(ps[:, banks + b, :], xs[0][:, u, kt, :], w[1][:, kt, c], start=False,
                                        stop=kt == KT - 1)
                ins.then_inc(done, 1)

            def turn_tile(st, u):
                pe.wait_ge(xn_ready, ST + st + 1)
                pe.wait_ge(xT_ready, ST + st - 1)
                for k in range(KT):
                    ins = pe.transpose(ps[:, 6 + u, k * P:(k + 1) * P], xn[:, u, k * P:(k + 1) * P], ident[:, :])
                ins.then_inc(xn_turned, 1)

            def project_qkv(st, u):
                pe.wait_ge(xT_ready, ST + st + 1)
                pe.wait_ge(qkv_taken, st + 1)
                project(u, wqkv, 3 * E, 3 * u, xs_used)

            turn_tile(0, 0)
            pe.wait_ge(raw_split, KT)
            pe.wait_ge(x_updated, ST)
            with pe.Fori(0, ST // 2 - 1) as i:
                for u in range(2):
                    turn_tile(2 * i + u + 1, 1 - u)
                    project_qkv(2 * i + u, u)
            turn_tile(ST - 1, 1)
            project_qkv(ST - 2, 0)
            project_qkv(ST - 1, 1)

            pe.wait_ge(qkv_taken, ST + CREDIT)
            pe.wait_ge(const_set, 4)

            def attend(plan, g, u):
                side = 0
                order = sides_of(plan)

                def wait_taken(engine, count):
                    pe.wait_ge(side_taken[engine], sides_before(g, engine) + count)

                def wait_side_bank():
                    if side >= SIDE_BANKS:
                        last = side - SIDE_BANKS
                        wait_taken(order[last], order[:last + 1].count(order[last]))
                    elif side == 0 and not leading(g):
                        for engine in side_taken:
                            wait_taken(engine, 0)

                def wait_turns(names):
                    at = [k for k, (kind, n, _) in enumerate(e for e in plan if e[0] in SIDE_KINDS)
                          if kind == "turn" and TURNS[n] in names]
                    for engine in side_taken:
                        last = [k for k in at if order[k] == engine]
                        if last:
                            wait_taken(engine, order[:last[-1] + 1].count(engine))

                for kind, n, rel in plan:
                    bank = SIDE_BANK + side % SIDE_BANKS
                    if kind == "turn":
                        operand, pair, half = TURNS[n]
                        if operand == "k":
                            pe.wait_ge(k_stacked, 2 * (g + 2))
                        elif operand == "q":
                            pe.wait_ge(q_stacked, 2 * (g + 2))
                        else:
                            pe.wait_ge(max_stacked, 4 * (g + 1) + 2 * half + 2)
                        wait_side_bank()
                        stack = stack_k if operand == "k" else stack_q
                        for t in range(HT):
                            src = stack[:, half * HT + t, 2 * pair:2 * pair + 2, :].rearrange("p j d -> p (j d)")
                            ins = pe.transpose(ps[:, bank, t * P:(t + 1) * P], src, ident[:, :])
                        ins.then_inc(side_ready, 1)
                    if kind == "max":
                        st, c, width, heads = MAX_TILES[n]
                        if n == 0:
                            wait_turns([(operand, pair, 0) for operand in "kq" for pair in range(2)])
                        if n == NMAX_LOW:
                            wait_turns([(operand, pair, 1) for operand in "kq" for pair in range(2)])
                        wait_side_bank()
                        diagonal = c + width == (st + 1) * P
                        for h, j in enumerate(heads):
                            rows = slice(j % 2 * SLOT, j % 2 * SLOT + KA)
                            end = (h + 1) * width
                            ins = pe.matmul(ps[:, bank, end - width:end], qT[rows, j // 2, st * P:(st + 1) * P],
                                            kT[1 - u][rows, j // 2, c:c + width], start=True, stop=not diagonal,
                                            tile_position=(j % 2 * SLOT, 0))
                            if diagonal:
                                ins = pe.matmul(ps[:, bank, end - P:end], ident_bf16[:, :], causal_mask[:, :],
                                                start=False, stop=True)
                        ins.then_inc(side_ready, 1)
                    if kind == "score":
                        half, kt = PV_STEPS[n // 2]
                        c = first_col(half, kt)
                        pair = n % 2
                        if n == 0:
                            for engine in side_taken:
                                wait_taken(engine, -1)
                        if n == 2 * HT:
                            for engine in side_taken:
                                wait_taken(engine, 0)
                        pe.wait_ge(exp_done, 2 * NPV * g + n + 1)
                        for j in range(2):
                            rows = slice(j * SLOT, j * SLOT + KB)
                            ins = pe.matmul(ps[:, 2 * pair + j, c:HALF], kT[u][rows, pair, kt * P:(kt + 1) * P],
                                            qTm[u][rows, pair, half * HALF + c:(half + 1) * HALF], start=True, stop=True,
                                            tile_position=(j * SLOT, 0))
                        ins.then_inc(scored, 1)
                    if kind == "pv":
                        half, kt = PV_STEPS[n]
                        c = first_col(half, kt)
                        gc, uc = g + rel, u if rel == 0 else 1 - u
                        if n == 0:
                            pe.wait_ge(v_staged, gc + 1)
                        if kt == 0:
                            pe.wait_ge(ctxT_taken, 2 * gc + half + 1)
                        if DIAG[n]:
                            pe.wait_ge(diag_masked, 2 * NDIAG * gc + 2 * sum(DIAG[:n + 1]))
                        pe.wait_ge(exp_done, 2 * NPV * gc + 2 * n + 2 + CREDIT)
                        for j in range(GH):
                            ins = pe.matmul(ps[32 * j:32 * (j + 1), PV_BANK, c:HALF], v_ext[uc][:, kt, j, :],
                                            probs[n % 2][j // 2][:, j % 2, c:HALF], start=kt == 0,
                                            stop=kt == (half + 1) * HT - 1, tile_position=(0, 32 * j))
                        ins.then_inc(pv_done, 1)
                    if kind == "turn_ctx":
                        pe.wait_ge(ctxT_taken, 2 * (g + rel) + n + 2)
                        wait_side_bank()
                        for t in range(HT):
                            ins = pe.transpose(ps[:, bank, t * P:(t + 1) * P], ctxT[:, t * P:(t + 1) * P], ident[:, :])
                        ins.then_inc(side_ready, 1)
                    if kind in SIDE_KINDS:
                        side += 1

            run_groups(pe, attend)

            def turn_ctx_tile(st, u):
                pe.wait_ge(ctx_lo, st + 1)
                for k in range(KT):
                    ins = pe.transpose(ps[:, 2 + u, k * P:(k + 1) * P], ctx_nat[:, st, k * P:(k + 1) * P], ident[:, :])
                ins.then_inc(ctx_turned, 1)

            pe.wait_ge(side_taken["dve"], sides_before(GROUPS, "dve") + 1)
            pe.wait_ge(raw_split, KT + 1)
            def project_context(st, u):
                pe.wait_ge(ctx_lo, st + 1 + CREDIT)
                pe.wait_ge(x_attended, st + 1)
                project(u, wo, E, u, projected)

            pe.sem_inc(projected, CREDIT)
            turn_ctx_tile(0, 0)
            for st in range(ST):
                if st + 1 < ST:
                    turn_ctx_tile(st + 1, (st + 1) % 2)
                project_context(st, st % 2)

            for st in range(ST):
                norm_turn(2 * ST + st)
            pe.wait_ge(xT_ready, 3 * ST)
            with pe.Fori(0, MT // 2) as i:
                for u in range(2):
                    gate_up(1, 2 * i + u, 2 * i + u, u, i + reload_count(CALL_UNITS + u))
            pe.wait_ge(hid_done, 4 * MT + CREDIT)
            for half in range(2):
                for p in range(DU):
                    n = MT + DU * half + p
                    down(half, n, n % 2, DU * (2 + half) + p + 1, reload_count(CALL_UNITS + n), p == 0, p == DU - 1)


_INPUTS = ["L0_attn_hidden_states", "L0_attn_qkv_w", "L0_attn_qkv_b", "L0_attn_out_w", "L0_attn_out_b",
           "L0_ffn_gate_q", "L0_ffn_gate_absmax", "L0_ffn_up_q", "L0_ffn_up_absmax", "L0_ffn_down_q",
           "L0_ffn_down_absmax"]


def _constants(seq, head_dim):
    import numpy as np
    half = head_dim // 2
    inv_freq = np.float32(1.0) / np.float32(10000.0) ** (np.arange(half, dtype=np.float32) / np.float32(half))
    ang = np.arange(seq, dtype=np.float32)[:, None] * inv_freq[None, :].astype(np.float32)
    cos, sin = np.cos(ang).astype(np.float32), np.sin(ang).astype(np.float32)
    return {
        "rope_cos": np.concatenate([cos, cos], 1),
        "rope_sin": np.concatenate([-sin, sin], 1),
        "identity": np.eye(P, dtype=np.float32),
    }


def kernel(**inputs):
    import numpy as np
    import concourse.bacc as bacc
    from concourse.bass_utils import run_bass_kernel_spmd

    nc = bacc.Bacc("TRN2", target_bir_lowering=False, num_devices=1)
    shape = inputs["L0_attn_hidden_states"].shape
    named = [(n, np.ascontiguousarray(inputs[n])) for n in _INPUTS]
    named += list(_constants(shape[1], shape[2] // HEADS).items())
    arrays, args = {}, []
    for name, a in named:
        arrays[f"in_{name}"] = a
        args.append(nc.dram_tensor(f"in_{name}", a.shape, mybir.dt.from_np(a.dtype), kind="ExternalInput").ap())
    args.append(nc.dram_tensor("out_0", shape, F32, kind="ExternalOutput").ap())
    macaron_block(nc, *args)
    r = run_bass_kernel_spmd(nc, [arrays], core_ids=[0])
    return r.results[0]["out_0"]
```

```python
from contextlib import ExitStack

import concourse.bass as bass
from concourse import mybir
from concourse.alu_op_type import AluOpType as ALU

ACT = mybir.ActivationFunctionType
AX = mybir.AxisListType
F32 = mybir.dt.float32
F32R = mybir.dt.float32r
BF16 = mybir.dt.bfloat16
I32 = mybir.dt.int32

P = 128
BANK = 512
HALF = 512
NF4_BLOCK = 64
HEADS = 32
EPS = 1e-5
MASKED = -66560.0 * 4
CREDIT = 2

NF4_LINES = {
    "n01": (0.30380716919898987, 1.1266502141952515),
    "n23": (0.1301555633544922, 0.12570475041866302),
    "n45": (0.09966795146465302, 0.014562468975782394),
    "p89": (0.08134990185499191, -0.0017696027643978596),
    "p1011": (0.0918029323220253, -0.029296500608325005),
    "p1213": (0.12190717458724976, -0.16882605850696564),
    "p1415": (0.2770431637763977, -1.2163453102111816),
}
NF4_SLOPE_67 = 0.09105003625154495
LINE_ORDER = ["p1011", "p1213", "n23", "n45", "p1415", "n01", "p89"]
LINE_SLOT = {name: n for n, name in enumerate(LINE_ORDER)}
LINES = len(LINE_ORDER)
MERGES = 6


def macaron_block(nc, x, qkv_w, qkv_b, out_w, out_b, gate_q, gate_absmax, up_q, up_absmax,
                  down_q, down_absmax, rope_cos, rope_sin, identity, out):
    S, E = x.shape[1], x.shape[2]
    M = gate_q.shape[0]
    ST = S // P
    HT = ST // 2
    KT = E // P
    MT = M // P
    DU = MT // 2
    UNITS = MT + DU
    CALL_UNITS = MT + 2 * DU
    D = E // HEADS
    GH = 4
    GROUPS = HEADS // GH
    GW = GH * D
    SLOT = 64
    KA = 3 * D
    KB = KA + 2

    with ExitStack() as top:
        def sem(name):
            return top.enter_context(nc.semaphore(name))

        def sb(ctx, name, shape, dt):
            return ctx.enter_context(nc.sbuf_tensor(name, shape, dt))

        xres = sb(top, "xres", [P, ST, E], F32)
        ident = sb(top, "ident", [P, P], F32)
        causal_mask = sb(top, "causal_mask", [P, P], BF16)
        ident_bf16 = sb(top, "ident_bf16", [P, P], BF16)
        cos_t = sb(top, "cos_t", [P, ST, D], F32)
        sin_t = sb(top, "sin_t", [P, ST, D], F32)
        absmax_gu = sb(top, "absmax_gu", [P, 2, MT, E // NF4_BLOCK], F32)
        absmax_d = sb(top, "absmax_d", [P, KT, M // NF4_BLOCK], F32)
        qkv_bias = sb(top, "qkv_bias", [P, 3 * E], F32)
        out_bias = sb(top, "out_bias", [P, E], F32)
        xn = sb(top, "xn", [P, 2, E], F32)
        stats = sb(top, "stats", [P, ST, 6], F32)
        moments = sb(top, "moments", [P, ST, 2], F32)
        minus_half = sb(top, "minus_half", [P, HT], F32)
        rstd_tmp = sb(top, "rstd_tmp", [P, 5, HT], F32)
        rstd = sb(top, "rstd", [P, ST], F32)

        with ExitStack() as ffn_mem:
            lines = sb(ffn_mem, "lines", [P, LINES, 1024], F32)
            xT_hi = sb(ffn_mem, "xT_hi", [P, KT, S], F32R)
            xT_lo = sb(ffn_mem, "xT_lo", [P, KT, S], F32R)
            codes = [sb(ffn_mem, f"codes{n}", [P, 1024], I32) for n in range(2)]
            t_code = sb(ffn_mem, "t_code", [P, 2, 1024], BF16)
            t_neg = sb(ffn_mem, "t_neg", [P, 2, 1024], BF16)
            w_scaled = sb(ffn_mem, "w_scaled", [P, 1024], F32)
            wT = [sb(ffn_mem, f"wT{n}", [P, 2, 1024], F32R) for n in range(2)]
            hs = [sb(ffn_mem, f"hs{n}", [P, 2, 2, HALF], F32R) for n in range(2)]
            silu_g = sb(ffn_mem, "silu_g", [P, 2, HALF], F32)
            hid = sb(ffn_mem, "hid", [P, MT, S], F32)

        with ExitStack() as proj_mem:
            raw_w = sb(proj_mem, "raw_w", [P, KT, 3 * E], F32)
            wqkv = [sb(proj_mem, f"wqkv_{part}", [P, KT, 3 * E], F32R) for part in ("hi", "lo")]
            xs = [sb(proj_mem, f"xs_{part}", [P, 2, KT, P], F32R) for part in ("hi", "lo")]
            q_biased = sb(proj_mem, "q_biased", [P, E], F32)
            k_biased = sb(proj_mem, "k_biased", [P, E], F32)
            q_swapped = sb(proj_mem, "q_swapped", [P, E], F32)
            k_swapped = sb(proj_mem, "k_swapped", [P, E], F32)

        with ExitStack() as attn_mem:
            stack_q = sb(attn_mem, "stack_q", [P, ST, GH, SLOT], F32)
            stack_k = sb(attn_mem, "stack_k", [P, ST, GH, SLOT], F32)
            qT = sb(attn_mem, "qT", [P, 2, S], F32R)
            qTm = [sb(attn_mem, f"qTm{n}", [P, 2, S], F32R) for n in range(2)]
            kT = [sb(attn_mem, f"kT{n}", [P, 2, S], F32R) for n in range(2)]
            probs = [[sb(attn_mem, f"probs{a}{b}", [P, 2, HALF], F32) for b in range(2)] for a in range(2)]
            v_ext = [sb(attn_mem, f"v_ext{n}", [P, ST, GH, 32], F32) for n in range(2)]
            ctxT = sb(attn_mem, "ctxT", [P, HALF], F32)
            maxima = sb(attn_mem, "maxima", [P, 2, ST, GH], F32)
            row_max = sb(attn_mem, "row_max", [P, ST, GH], F32)
            inv_den = sb(attn_mem, "inv_den", [P, 2, HT, GH], F32)
            raw_wo = sb(attn_mem, "raw_wo", [P, KT, E], F32)
            q_nat = sb(attn_mem, "q_nat", [P, ST, E], F32)
            k_nat = sb(attn_mem, "k_nat", [P, ST, E], F32)
            v_nat = sb(attn_mem, "v_nat", [P, ST, E], F32)
            ctx_nat = sb(attn_mem, "ctx_nat", [P, ST, E], F32)
            wo = [sb(attn_mem, f"wo_{part}", [P, KT, E], F32R) for part in ("hi", "lo")]

        ps = top.enter_context(nc.psum_tensor("ps", [P, 8, BANK], F32))

        scratch = nc.dram_tensor("weights_split", (UNITS, P, 2, 1024), F32, kind="Internal").ap()

        x_loaded = [sem(f"x_loaded{n}") for n in range(2)]
        first_loaded = sem("first_loaded")
        consts_loaded = sem("consts_loaded")
        codes_loaded = [sem(f"codes_loaded{n}") for n in range(2)]
        t_ready = sem("t_ready")
        t_neg_ready = sem("t_neg_ready")
        lines_ready = sem("lines_ready")
        merged = sem("merged")
        summed = sem("summed")
        w_ready = sem("w_ready")
        w_turned = sem("w_turned")
        hi_ready = sem("hi_ready")
        lo_ready = sem("lo_ready")
        spilled = [sem(f"spilled{n}") for n in range(2)]
        reloaded = [sem(f"reloaded{n}") for n in range(2)]
        down_used = sem("down_used")
        gate_done = sem("gate_done")
        up_done = sem("up_done")
        silu_done = sem("silu_done")
        hid_done = sem("hid_done")
        hs_hi_ready = sem("hs_hi_ready")
        first_hs_ready = sem("first_hs_ready")
        hs_ready = sem("hs_ready")
        x_updated = sem("x_updated")
        const_set = sem("const_set")
        maxima_set = sem("maxima_set")
        waits_passed = sem("waits_passed")
        norm_stats = sem("norm_stats")
        norm_moments = sem("norm_moments")
        rstd_step = sem("rstd_step")
        rstd_ready = sem("rstd_ready")
        xn_ready = sem("xn_ready")
        xn_turned = sem("xn_turned")
        xT_hi_ready = sem("xT_hi_ready")
        xT_ready = sem("xT_ready")
        stored = sem("stored")
        raw_loaded = [sem(f"wqkv_loaded{c}") for c in range(KT)]
        wo_loaded = sem("wo_loaded")
        wo_hi_ready = sem("wo_hi_ready")
        wo_split = sem("wo_split")
        raw_hi = sem("raw_hi")
        raw_split = sem("raw_split")
        xs_used = sem("xs_used")
        qkv_taken = sem("qkv_taken")
        qk_biased = sem("qk_biased")
        k_rope = sem("k_rope")
        q_rope = sem("q_rope")
        pads_set = sem("pads_set")
        stack_hi = sem("stack_hi")
        q_stacked = sem("q_stacked")
        k_stacked = sem("k_stacked")
        v_staged = sem("v_staged")
        side_ready = sem("side_ready")
        side_taken = {"act": sem("side_taken_act"), "dve": sem("side_taken_dve")}
        row_max_step = sem("row_max_step")
        max_stacked = sem("max_stacked")
        scored = sem("scored")
        exp_done = sem("exp_done")
        diag_masked = sem("diag_masked")
        pv_done = sem("pv_done")
        ctxT_taken = sem("ctxT_taken")
        inverted = sem("inverted")
        ctx_turned = sem("ctx_turned")
        ctx_hi = sem("ctx_hi")
        ctx_lo = sem("ctx_lo")
        projected = sem("projected")
        bias_added = sem("bias_added")
        x_attended = sem("x_attended")

        PV_STEPS = [(half, kt) for half in range(2) for kt in range((half + 1) * HT)]
        NPV = len(PV_STEPS)
        DIAG = [kt * P >= half * HALF for half, kt in PV_STEPS]
        NDIAG = sum(DIAG)

        def first_col(half, kt):
            return max(0, kt * P - half * HALF)

        MAX_TILES = []
        for st in range(ST):
            for c in range(0, (st + 1) * P, BANK):
                width = min((st + 1) * P - c, BANK)
                for r in range(2):
                    heads = list(range(r, GH, 2))
                    MAX_TILES += [(st, c, width, heads)] if 2 * width <= BANK else [(st, c, width, [j]) for j in heads]
        NMAX = len(MAX_TILES)
        NMAX_LOW = len([tile for tile in MAX_TILES if tile[0] < HT])

        TURNS = [(operand, pair, half) for half in range(2) for operand in "kq" for pair in range(2)]
        TURNS += [("m", pair, half) for half in range(2) for pair in range(2)]

        SIDE_KINDS = ("turn", "max", "turn_ctx")
        SIDE_BANK, SIDE_BANKS, PV_BANK = 5, 3, 4
        TAIL, TAIL_STEPS = 8, 2
        SIDE_STEP = 3
        STEP_COLUMNS = 43

        def side_work():
            turns = [("turn", n, 1) for n in range(len(TURNS))]
            maxs = [("max", n, 1) for n in range(NMAX)]
            items = turns[0:4] + maxs[0:2] + turns[4:8] + maxs[2:NMAX_LOW] + [("stack_max", 0, 1)]
            items += maxs[NMAX_LOW:NMAX_LOW + 3] + turns[8:10] + maxs[NMAX_LOW + 3:NMAX - TAIL]

            def columns(item):
                if item[0] == "stack_max":
                    return BANK
                return len(MAX_TILES[item[1]][3]) * MAX_TILES[item[1]][2] + 64 if item[0] == "max" else BANK

            steps = [0] * SIDE_STEP + [HALF - first_col(half, kt) + STEP_COLUMNS for half, kt in PV_STEPS[SIDE_STEP:]]
            work = [[] for _ in range(NPV)]
            total, done, n = sum(columns(item) for item in items), 0, SIDE_STEP
            for item in items:
                while n < NPV - 1 and done * sum(steps) >= total * sum(steps[:n + 1]):
                    n += 1
                work[n].append(item)
                done += columns(item)
            return work

        def group_plan(before, this, following):
            work = side_work() if following else [[]] * NPV
            plan = [("stack", 0, 1)] if following and not this else []
            for n in range(NPV):
                side = list(work[n])
                if this and n < TAIL_STEPS:
                    side += [("max", k, 0) for k in range(NMAX - TAIL + n * TAIL // TAIL_STEPS,
                                                          NMAX - TAIL + (n + 1) * TAIL // TAIL_STEPS)]
                    if n == TAIL_STEPS - 1:
                        side.append(("stack_max", 1, 0))
                if before and n == 1:
                    side.append(("turn_ctx", 1, -1))
                if this and n == HT + 2:
                    side.append(("turn_ctx", 0, 0))
                a, b = -(-len(side) // 3), -(-2 * len(side) // 3)
                if this:
                    plan.append(("score", 2 * n, 0))
                plan += side[:a]
                if this:
                    plan.append(("score", 2 * n + 1, 0))
                plan += side[a:b]
                if this and n == TAIL_STEPS:
                    plan += [("turn", 10, 0), ("turn", 11, 0)]
                    if following:
                        plan.append(("stack", 0, 1))
                if this and n >= 1:
                    plan.append(("pv", n - 1, 0))
                if before and n == 0:
                    plan += [("pv", NPV - 1, -1), ("take_ctx", 1, -1)]
                if this and n == HT:
                    plan.append(("take_ctx", 0, 0))
                if following and n == 1:
                    plan.append(("stage_v", 0, 1))
                plan += side[b:]
            return plan

        def side_engine(kind, n):
            return "act" if kind == "turn" and n % 4 < 3 else "dve"

        def sides_of(plan):
            return [side_engine(kind, n) for kind, n, _ in plan if kind in SIDE_KINDS]

        LEAD_PLAN, FIRST_PLAN = group_plan(False, False, True), group_plan(False, True, True)
        BODY_PLAN, LAST_PLAN = group_plan(True, True, True), group_plan(True, True, False)
        END_PLAN = [("pv", NPV - 1, -1), ("take_ctx", 1, -1), ("turn_ctx", 1, -1)]

        def leading(g):
            return isinstance(g, int) and g < 0

        def wait_apart(eng, signal, count):
            eng.wait_ge(signal, count)
            eng.sem_inc(waits_passed, 1)

        def sides_before(g, engine=None):
            def of(plan):
                return len([e for e in sides_of(plan) if engine in (None, e)])

            if isinstance(g, int) and g <= 0:
                return of(LEAD_PLAN) * (g + 1)
            before = of(LEAD_PLAN) + of(FIRST_PLAN)
            if isinstance(g, int) and g == GROUPS:
                return before + of(BODY_PLAN) * (g - 2) + of(LAST_PLAN)
            return before + of(BODY_PLAN) * (g - 1)

        def run_groups(eng, run_plan):
            run_plan(LEAD_PLAN, -1, 1)
            run_plan(FIRST_PLAN, 0, 0)
            with eng.Fori(0, GROUPS // 2 - 1) as i:
                for u in range(2):
                    run_plan(BODY_PLAN, 2 * i + 1 + u, 1 - u)
            run_plan(LAST_PLAN, GROUPS - 1, 1)
            run_plan(END_PLAN, GROUPS, 0)

        x_dram = x[0].rearrange("(t p) e -> p t e", p=P)
        out_dram = out[0].rearrange("(t p) e -> p t e", p=P)
        down_dram = down_q.rearrange("(c p) m -> p c m", p=P)

        FIRST_CONSTS, CONSTS = 3, 5

        def wait_unit_free(eng, call, n):
            if isinstance(n, int) and n >= MT + 2:
                eng.wait_ge(down_used, 2 * DU * call + n - MT - 1)
            elif isinstance(n, int) and n < 2 and call > 0:
                eng.wait_ge(down_used, 2 * DU * call + n - 1)
            else:
                eng.wait_ge(up_done, 2 * MT * call + 2 * n + 2)

        def reload_count(v):
            first = UNITS + (v - UNITS) % 2
            return (v - first) // 2 + 1

        def rope(eng, nat, biased, swapped, st, ready, steps):
            dst = nat[:, bass.ds(st, 1), :].rearrange("p a (h t d) -> p (a h) t d", t=2, d=D // 2)
            src = biased[:, :].rearrange("p (h t d) -> p h t d", t=2, d=D // 2)
            tmp = swapped[:, :].rearrange("p (h t d) -> p h t d", t=2, d=D // 2)
            cos, sin = (tab[:, bass.ds(st, 1), :].rearrange("p a (t d) -> p a t d", t=2)
                        .broadcast_to([P, HEADS, 2, D // 2]) for tab in (cos_t, sin_t))
            wait_apart(eng, *ready)
            eng.tensor_tensor(dst, src, cos, ALU.mult).then_inc(steps, 1)
            eng.tensor_tensor(tmp, src[:, :, ::-1, :], sin, ALU.mult).then_inc(steps, 1)
            wait_apart(eng, steps, 3 * st + 3)
            eng.tensor_tensor(dst, dst, tmp, ALU.add).then_inc(steps, 1)

        def hs_lo(eng, k, u, half, p, ready):
            eng.wait_ge(hs_hi_ready, k)
            eng.tensor_tensor(hs[u][:, 1, :, :], hid[:, 2 * p:2 * p + 2, half * HALF:(half + 1) * HALF],
                              hs[u][:, 0, :, :].bitcast(F32), ALU.subtract).then_inc(ready, 1)

        def take_turn(eng, n, u, bank):
            operand, pair, half = TURNS[n]
            dst = {"k": kT[u], "q": qT, "m": qTm[u]}[operand][:, pair, half * HALF:(half + 1) * HALF]
            if side_engine("turn", n) == "act":
                eng.activation(dst, ps[:, bank, :], ACT.Copy).then_inc(side_taken["act"], 1)
            else:
                eng.tensor_copy(dst, ps[:, bank, :]).then_inc(side_taken["dve"], 1)

        block = top.enter_context(nc.Block())

        @block.sync
        def _(sp):
            def load_gate_up(s, u, k):
                cv = codes[u][:, :].rearrange("p (a e) -> p a e", a=2)
                sp.dma_start(cv[:, 0:1, :], gate_q.rearrange("(t p) e -> p t e", p=P)[:, bass.ds(s, 1), :]
                             ).then_inc(codes_loaded[u], 16)
                sp.dma_start(cv[:, 1:2, :], up_q.rearrange("(t p) e -> p t e", p=P)[:, bass.ds(s, 1), :]
                             ).then_inc(codes_loaded[u], 16)

            def load_down(p, u):
                cv = codes[u][:, :].rearrange("p (c m) -> p c m", c=KT)
                for c in range(0, KT, 2):
                    sp.dma_start(cv[:, c:c + 2, :], down_dram[:, c:c + 2, bass.ds(2 * P * p, 2 * P)]
                                 ).then_inc(codes_loaded[u], 16)

            def spill(s, u):
                sp.wait_ge(lo_ready, s + 2)
                sp.dma_start(scratch[bass.ds(s, 1)].rearrange("a p h n -> (a p) h n"), wT[u][:, :, :].bitcast(F32)
                             ).then_inc(spilled[u], 16)

            def reload(s, call, n, u):
                wait_unit_free(sp, call, n)
                sp.dma_start(wT[u][:, :, :].bitcast(F32), scratch[bass.ds(s, 1)].rearrange("a p h n -> (a p) h n")
                             ).then_inc(reloaded[u], 16)

            for n in range(2):
                sp.sem_inc(spilled[n], 16)
            load_gate_up(0, 0, 1)
            sp.dma_start(xres[:, 0:HT, :], x_dram[:, 0:HT, :]).then_inc(x_loaded[0], 16)
            sp.dma_start(xres[:, HT:ST, :], x_dram[:, HT:ST, :]).then_inc(x_loaded[1], 16)
            sp.dma_start(ident[:, :], identity).then_inc(first_loaded, 16)
            sp.dma_start(absmax_gu[:, 0], gate_absmax.rearrange("(t p b) -> p t b", p=P, t=MT)).then_inc(first_loaded, 16)
            sp.dma_start(absmax_gu[:, 1], up_absmax.rearrange("(t p b) -> p t b", p=P, t=MT)).then_inc(first_loaded, 16)
            load_gate_up(1, 1, 1)
            sp.dma_start(absmax_d[:, :, :], down_absmax.rearrange("(c p b) -> p c b", p=P, c=KT)).then_inc(consts_loaded, 16)
            sp.dma_start(cos_t[:, :, :], rope_cos.rearrange("(t p) d -> p t d", p=P)).then_inc(consts_loaded, 16)
            sp.dma_start(sin_t[:, :, :], rope_sin.rearrange("(t p) d -> p t d", p=P)).then_inc(consts_loaded, 16)
            sp.dma_start(qkv_bias[:, :], qkv_b.rearrange("(a n) -> a n", a=1).broadcast_to([P, 3 * E])).then_inc(consts_loaded, 16)
            sp.dma_start(out_bias[:, :], out_b.rearrange("(a n) -> a n", a=1).broadcast_to([P, E])).then_inc(consts_loaded, 16)
            with sp.Fori(0, MT // 2 - 1) as i:
                for u in range(2):
                    s = 2 * i + u
                    sp.wait_ge(t_ready, s + 1)
                    load_gate_up(s + 2, u, i + 2)
                    spill(s, u)
            for s in range(MT - 2, UNITS):
                if s + 2 < UNITS:
                    sp.wait_ge(t_ready, s + 1)
                    load_down(s + 2 - MT, s % 2)
                spill(s, s % 2)
            for p in range(DU):
                v = MT + p
                sp.wait_ge(spilled[v % 2], 16 + 16 * (v // 2 + 1))
                reload(v, 0, UNITS + p, (UNITS + p) % 2)
                if 1 <= p <= KT:
                    sp.wait_ge(summed, UNITS + 1)
                    sp.dma_start(raw_w[:, p - 1, :], qkv_w[(p - 1) * P:p * P, :]).then_inc(raw_loaded[p - 1], 16)
            sp.wait_ge(k_rope, 3 * ST + 1)
            sp.wait_ge(q_rope, 3 * ST + 1)
            sp.dma_start(raw_wo[:, :, :], out_w.rearrange("(c p) n -> p c n", p=P)).then_inc(wo_loaded, 16)

            sp.wait_ge(projected, 1 + CREDIT)
            for n in range(2):
                reload(n, 1, n, n)
            with sp.Fori(0, MT // 2 - 1) as i:
                for u in range(2):
                    reload(2 * i + u + 2, 1, 2 * i + u + 2, u)
            for p in range(DU):
                reload(MT + p, 1, MT + p, (MT + p) % 2)
            for p in range(DU):
                reload(MT + p, 1, UNITS + p, (UNITS + p) % 2)

            sp.wait_ge(x_updated, ST + HT)
            sp.dma_start(out_dram[:, HT:ST, :], xres[:, HT:ST, :]).then_inc(stored, 16)
            for t in reversed(range(HT)):
                sp.wait_ge(x_updated, 2 * ST - t)
                sp.dma_start(out_dram[:, t, :], xres[:, t, :]).then_inc(stored, 16)
            sp.wait_ge(stored, 16 * (HT + 1))

        @block.gpsimd
        def _(pool):
            def shift_codes(s, u, k):
                wait_apart(pool, codes_loaded[u], 32 * k)
                pool.tensor_scalar(t_code[:, u, :], codes[u][:, :], 1.0, -7.0, ALU.mult, ALU.add).then_inc(t_ready, 1)

            def scale_unit(s, absmax, shape):
                pool.wait_ge(merged, MERGES * (s + 2))
                pool.wait_ge(w_turned, s + 1)
                pool.tensor_tensor(w_scaled[:, :], lines[:, LINE_SLOT["n01"], :], lines[:, LINE_SLOT["p89"], :],
                                   ALU.add).then_inc(summed, 1)
                pool.wait_ge(summed, s + 2)
                wv = w_scaled[:, :].rearrange("p (a b n) -> p a b n", a=shape[0], b=shape[1])
                pool.tensor_tensor(wv, wv, absmax.unsqueeze(3).broadcast_to([P, *shape, NF4_BLOCK]),
                                   ALU.mult).then_inc(w_ready, 1)

            def scale_gate_up(s):
                scale_unit(s, absmax_gu[:, :, bass.ds(s, 1), :].rearrange("p a t b -> p a (t b)"), (2, E // NF4_BLOCK))

            def scale_down(s):
                scale_unit(s, absmax_d[:, :, bass.ds(4 * (s - MT), 4)], (KT, 2 * P // NF4_BLOCK))

            def inverse_deviation(half, first):
                pool.wait_ge(norm_moments, first + ST // 2 * (half + 1))
                a, b = half * HT, (half + 1) * HT
                base = rstd_steps[0]

                def step(ins):
                    rstd_steps[0] += 1
                    ins.then_inc(rstd_step, 1)
                    pool.wait_ge(rstd_step, rstd_steps[0])

                ve, r, rr, c = (rstd_tmp[:, n, :] for n in range(4))
                step(pool.tensor_scalar(ve, moments[:, a:b, 1], 1.0, EPS, ALU.mult, ALU.add))
                step(pool.tensor_tensor(r, ve, minus_half[:, :], ALU.pow))
                step(pool.tensor_tensor(rr, r, r, ALU.mult))
                step(pool.tensor_tensor(c, rr, ve, ALU.mult))
                step(pool.tensor_scalar(rr, c, -0.5, 1.5, ALU.mult, ALU.add))
                pool.tensor_tensor(rstd[:, a:b], r, rr, ALU.mult).then_inc(rstd_ready, 1)

            rstd_steps = [0]
            pool.memset(minus_half[:, :], -0.5).then_inc(const_set, 1)
            pool.memset(causal_mask[:, :], 0.0).then_inc(const_set, 1)
            pool.wait_ge(const_set, 2)
            pool.affine_select(out=causal_mask[:, :], in_=causal_mask[:, :], compare_op=ALU.is_ge,
                               fill=MASKED, base=0, pattern=[[-1, P]], channel_multiplier=1).then_inc(const_set, 1)
            pool.sem_inc(summed, 1)
            pool.wait_ge(const_set, 3)
            shift_codes(0, 0, 1)
            inverse_deviation(0, 0)
            inverse_deviation(1, 0)
            shift_codes(1, 1, 1)
            pool.wait_ge(first_loaded, 16 * FIRST_CONSTS)
            pool.tensor_copy(ident_bf16[:, :], ident[:, :]).then_inc(const_set, 1)
            with pool.Fori(0, MT // 2 - 1) as i:
                for u in range(2):
                    scale_gate_up(2 * i + u)
                    shift_codes(2 * i + u + 2, u, i + 2)
            pool.wait_ge(consts_loaded, 16 * CONSTS)
            for s in range(MT - 2, UNITS):
                (scale_gate_up if s < MT else scale_down)(s)
                if s + 2 < UNITS:
                    shift_codes(s + 2, s % 2, (s + 2) // 2 + 1)
                if s > MT:
                    hs_lo(pool, s - MT, (s - 1) % 2, 0, s - MT - 1, first_hs_ready)
            hs_lo(pool, DU, (UNITS - 1) % 2, 0, DU - 1, first_hs_ready)

            for half in range(2):
                inverse_deviation(half, ST)

            pool.wait_ge(raw_split, KT)
            pool.memset(stack_k[:, :, :, KA:KB], 1.0).then_inc(pads_set, 1)
            pool.memset(stack_k[:, :, :, KB:SLOT], 0.0).then_inc(pads_set, 1)
            pool.memset(stack_q[:, :, :, KA:SLOT], 0.0).then_inc(pads_set, 1)
            pool.sem_inc(q_rope, 1)
            with pool.Fori(0, ST) as st:
                rope(pool, q_nat, q_biased, q_swapped, st, (qk_biased, 2 * st + 1), q_rope)

            pool.wait_ge(xn_ready, 2 * ST)
            pool.wait_ge(xs_used, ST + CREDIT)
            pool.wait_ge(k_rope, 3 * ST + 1)
            pool.wait_ge(q_rope, 3 * ST + 1)
            for n in range(2):
                pool.memset(v_ext[n][:, :, :, D:D + 1], 1.0).then_inc(pads_set, 1)
                pool.memset(v_ext[n][:, :, :, D + 1:32], 0.0).then_inc(pads_set, 1)

            def attend(plan, g, u):
                for kind, n, rel in plan:
                    if kind == "stack":
                        qg = q_nat[:, :, bass.ds((g + 1) * GW, GW)].rearrange("p t (j d) -> p t j d", j=GH)
                        wait_apart(pool, stack_hi, 2 * (g + 1) + 2)
                        pool.tensor_tensor(stack_q[:, :, :, D:2 * D], qg, stack_q[:, :, :, 0:D], ALU.subtract
                                           ).then_inc(q_stacked, 1)
                        pool.tensor_scalar(stack_q[:, :, :, 2 * D:3 * D], stack_q[:, :, :, 0:D], 1.0, 0.0, ALU.mult,
                                           ALU.add).then_inc(q_stacked, 1)
                    if kind == "pv" and plan is FIRST_PLAN and HT <= n + 1 < HT + KT:
                        c = n + 1 - HT
                        for st in (2 * c, 2 * c + 1):
                            pool.tensor_tensor(xres[:, st, :], xres[:, st, :], out_bias[:, :], ALU.add
                                               ).then_inc(bias_added, 1)
                        pool.wait_ge(wo_hi_ready, 1)
                        pool.tensor_tensor(wo[1][:, c, :], raw_wo[:, c, :], wo[0][:, c, :].bitcast(F32), ALU.subtract
                                           ).then_inc(wo_split, 1)
                    if kind == "score" and DIAG[n // 2]:
                        half, kt = PV_STEPS[n // 2]
                        c = first_col(half, kt)
                        tile = probs[n // 2 % 2][n % 2][:, :, c:c + P]
                        wait_apart(pool, exp_done, 2 * NPV * g + n + 1 + CREDIT)
                        pool.affine_select(out=tile, in_=tile, compare_op=ALU.is_ge, fill=0.0, base=0,
                                           pattern=[[0, 2], [1, P]], channel_multiplier=-1).then_inc(diag_masked, 1)

            run_groups(pool, attend)

            pool.wait_ge(consts_loaded, 16 * CONSTS)
            for half in range(2):
                inverse_deviation(half, 2 * ST)

        @block.scalar
        def _(act):
            def line(name, s, u, src):
                a, b = NF4_LINES[name]
                act.activation(lines[:, LINE_SLOT[name], :], src[:, u, :], ACT.Copy, bias=b, scale=a).then_inc(lines_ready, 1)

            def lines_first(s, u):
                act.wait_ge(t_ready, s + 1)
                act.wait_ge(merged, MERGES * s + 1)
                line("p1011", s, u, t_code)
                act.wait_ge(merged, MERGES * s + 3)
                line("p1213", s, u, t_code)
                act.wait_ge(t_neg_ready, s + 1)
                line("n23", s, u, t_neg)
                act.wait_ge(merged, MERGES * s + 5)
                line("n45", s, u, t_neg)

            def lines_last(s, u):
                act.wait_ge(merged, MERGES * s + 6)
                line("p1415", s, u, t_code)
                act.wait_ge(summed, s + 1)
                line("n01", s, u, t_neg)
                line("p89", s, u, t_code)

            def split_hi(s, u, k):
                act.wait_ge(w_turned, s + 2)
                wait_unit_free(act, 0, s)
                act.wait_ge(spilled[u], 16 * k)
                act.activation(wT[u][:, 0, :].rearrange("p (a n) -> p a n", a=2), ps[:, 4:6, :], ACT.Copy
                               ).then_inc(hi_ready, 1)

            def silu(call, mt, half):
                n = 2 * MT * call + 2 * mt + half
                act.wait_ge(gate_done, n + 1)
                act.wait_ge(hid_done, n + 1)
                act.activation(silu_g[:, half, :], ps[:, 2 * half, :], ACT.Silu).then_inc(silu_done, 1)

            def hs_hi(call, n, u, half, p):
                if n >= MT + 2:
                    act.wait_ge(down_used, 2 * DU * call + n - MT - 1)
                act.activation(hs[u][:, 0, :, :], hid[:, bass.ds(2 * p, 2), half * HALF:(half + 1) * HALF], ACT.Copy
                               ).then_inc(hs_hi_ready, 1)

            def norm_hi(n, st):
                act.wait_ge(xn_turned, n + 1)
                act.activation(xT_hi[:, :, st * P:(st + 1) * P], ps[:, 6 + n % 2, :].rearrange("p (k s) -> p k s", k=KT),
                               ACT.Copy).then_inc(xT_hi_ready, 1)

            act.sem_inc(exp_done, CREDIT)
            act.sem_inc(ctxT_taken, 1)
            act.preload_act_table(ACT.Silu)
            lines_first(0, 0)
            norm_hi(0, 0)
            norm_hi(1, 1)
            lines_last(0, 0)
            norm_hi(2, 2)
            norm_hi(3, 3)
            lines_first(1, 1)
            for st in range(HT, ST):
                norm_hi(st, st)
            split_hi(0, 0, 1)
            lines_last(1, 1)
            lines_first(2, 0)
            lines_last(2, 0)
            with act.Fori(0, MT // 2 - 1) as i:
                for w in range(2):
                    s, u = 2 * i + 1 + w, (1 + w) % 2
                    split_hi(s, u, i + 1 + w)
                    lines_first(s + 2, u)
                    silu(0, s - 1, 0)
                    lines_last(s + 2, u)
                    silu(0, s - 1, 1)
            for s in range(MT - 1, UNITS):
                u = s % 2
                split_hi(s, u, s // 2 + 1)
                if s >= MT:
                    act.wait_ge(hid_done, 4 * (s - MT + 1) + CREDIT)
                    hs_hi(0, s, u, 0, s - MT)
                if s + 2 < UNITS:
                    lines_first(s + 2, u)
                if s <= MT:
                    silu(0, s - 1, 0)
                if s + 2 < UNITS:
                    lines_last(s + 2, u)
                if s <= MT:
                    silu(0, s - 1, 1)
            for p in range(DU):
                v = UNITS + p
                hs_hi(0, v, v % 2, 1, p)
                if p >= DU - KT:
                    c = p - (DU - KT)
                    act.wait_ge(raw_loaded[c], 16)
                    act.activation(wqkv[0][:, c, :], raw_w[:, c, :], ACT.Copy).then_inc(raw_hi, 1)

            with act.Fori(0, ST // 2) as i:
                for u in range(2):
                    st = 2 * i + u
                    act.wait_ge(xn_turned, ST + st + 1)
                    act.wait_ge(xs_used, st + 1)
                    act.activation(xs[0][:, u, :, :], ps[:, 6 + u, :].rearrange("p (k s) -> p k s", k=KT), ACT.Copy
                                   ).then_inc(xT_hi_ready, 1)

            act.preload_act_table(ACT.Exp)

            def attend(plan, g, u):
                side = 0
                for kind, n, rel in plan:
                    if kind == "stack":
                        if not leading(g):
                            act.wait_ge(side_ready, sides_before(g) + side)
                        cols = bass.ds((g + 1) * GW, GW)
                        for nat, stack, steps in ((k_nat, stack_k, k_rope), (q_nat, stack_q, q_rope)):
                            if leading(g):
                                act.wait_ge(steps, 3 * ST + 1)
                            act.activation(stack[:, :, :, 0:D].bitcast(F32R),
                                           nat[:, :, cols].rearrange("p t (j d) -> p t j d", j=GH), ACT.Copy
                                           ).then_inc(stack_hi, 1)
                    if kind == "stage_v" and plan is FIRST_PLAN:
                        act.wait_ge(wo_loaded, 16)
                        act.activation(wo[0][:, :, :], raw_wo[:, :, :], ACT.Copy).then_inc(wo_hi_ready, 1)
                    if kind == "score":
                        half, kt = PV_STEPS[n // 2]
                        c = first_col(half, kt)
                        act.wait_ge(scored, 2 * NPV * g + n + 1)
                        act.wait_ge(pv_done, NPV * g + n // 2 + 1)
                        act.activation(probs[n // 2 % 2][n % 2][:, :, c:HALF], ps[:, 2 * (n % 2):2 * (n % 2) + 2, c:HALF],
                                       ACT.Exp, scale=float(D) ** -0.5).then_inc(exp_done, 1)
                    if kind == "take_ctx":
                        act.wait_ge(pv_done, NPV * (g + rel) + CREDIT + (NPV if n else HT))
                        if not isinstance(g, int) or 2 * (g + rel) + n > 0:
                            act.wait_ge(inverted, 2 * (g + rel) + n)
                        act.activation(ctxT[:, :], ps[:, PV_BANK, :], ACT.Copy).then_inc(ctxT_taken, 1)
                    if kind in SIDE_KINDS:
                        if side_engine(kind, n) == "act":
                            act.wait_ge(side_ready, sides_before(g) + side + 1)
                            take_turn(nc.scalar, n, 1 - u if rel else u, SIDE_BANK + side % SIDE_BANKS)
                        side += 1

            run_groups(act, attend)

            act.preload_act_table(ACT.Silu)

            def context_hi(st, u):
                act.wait_ge(ctx_turned, st + 1)
                act.wait_ge(projected, st + 1)
                act.activation(xs[0][:, u, :, :], ps[:, 2 + u, :].rearrange("p (k s) -> p k s", k=KT), ACT.Copy
                               ).then_inc(ctx_hi, 1)

            with act.Fori(0, ST // 2 - 1) as i:
                for u in range(2):
                    context_hi(2 * i + u, u)
            context_hi(ST - 2, 0)
            norm_hi(2 * ST, 0)
            context_hi(ST - 1, 1)
            for st in range(1, ST):
                norm_hi(2 * ST + st, st)

            def hs_high(q, p):
                n = MT + DU * q + p
                hs_hi(1, n, n % 2, 1 - q, p)

            with act.Fori(0, MT - 1) as mt:
                for half in range(2):
                    silu(1, mt, half)
            act.wait_ge(hid_done, 2 * MT + 8 + CREDIT)
            hs_high(0, 0)
            hs_high(0, 1)
            for half in range(2):
                silu(1, MT - 1, half)
            act.wait_ge(hid_done, 4 * MT + CREDIT)
            for q in range(2):
                for p in range(2 if q == 0 else 0, DU):
                    hs_high(q, p)

        @block.vector
        def _(dve):
            def slot(name):
                return lines[:, LINE_SLOT[name], :]

            def clamp_codes(s, u):
                dve.wait_ge(t_ready, s + 1)
                dve.tensor_scalar(t_neg[:, u, :], t_code[:, u, :], 0.0, None, ALU.min).then_inc(t_neg_ready, 1)

            def own(s, k):
                dve.wait_ge(merged, MERGES * (s + 1) + k)

            def merge_first(s):
                dve.wait_ge(lines_ready, LINES * s + 2)
                dve.tensor_tensor(slot("p1213"), slot("p1011"), slot("p1213"), ALU.max).then_inc(merged, 1)
                dve.wait_ge(lines_ready, LINES * s + 4)
                dve.tensor_tensor(slot("n45"), slot("n23"), slot("n45"), ALU.min).then_inc(merged, 1)

            def merge_last(s, u):
                dve.wait_ge(lines_ready, LINES * s + 5)
                own(s, 1)
                dve.tensor_tensor(slot("p1415"), slot("p1213"), slot("p1415"), ALU.max).then_inc(merged, 1)
                dve.wait_ge(lines_ready, LINES * s + 6)
                own(s, 2)
                dve.tensor_tensor(slot("n45"), slot("n01"), slot("n45"), ALU.min).then_inc(merged, 1)
                own(s, 4)
                dve.scalar_tensor_tensor(slot("n01"), t_neg[:, u, :], NF4_SLOPE_67, slot("n45"), ALU.mult, ALU.min
                                         ).then_inc(merged, 1)
                dve.wait_ge(lines_ready, LINES * s + 7)
                own(s, 3)
                dve.scalar_tensor_tensor(slot("p89"), slot("p1415"), 0.0, slot("p89"), ALU.max, ALU.max
                                         ).then_inc(merged, 1)

            def split_lo(s, u):
                dve.wait_ge(hi_ready, s + 1)
                dve.tensor_tensor(wT[u][:, 1, :].rearrange("p (a n) -> p a n", a=2), ps[:, 4:6, :],
                                  wT[u][:, 0, :].rearrange("p (a n) -> p a n", a=2).bitcast(F32), ALU.subtract
                                  ).then_inc(lo_ready, 1)

            def hidden(call, mt, half):
                n = 2 * MT * call + 2 * mt + half
                dve.wait_ge(silu_done, n + 1)
                dve.wait_ge(up_done, n + 5)
                dve.tensor_tensor(hid[:, bass.ds(mt, 1), half * HALF:(half + 1) * HALF].rearrange("p a n -> p (a n)"),
                                  silu_g[:, half, :], ps[:, 2 * half + 1, :], ALU.mult).then_inc(hid_done, 1)

            def add_down(n, half):
                dve.wait_ge(down_used, DU * (n + 1))
                for t in reversed(range(HT)):
                    st = half * HT + t
                    dve.scalar_tensor_tensor(xres[:, st, :], ps[:, 4 * half + t, :], 0.5, xres[:, st, :],
                                             ALU.mult, ALU.add).then_inc(x_updated, 1)

            def norm_statistics(n0, half):
                for st in range(half * HT, (half + 1) * HT):
                    dve.bn_stats(stats[:, st, :], xres[:, st, :]).then_inc(norm_stats, 1)
                for st in range(half * HT, (half + 1) * HT):
                    dve.wait_ge(norm_stats, n0 + st + 1)
                    dve.bn_aggr(moments[:, st, :], stats[:, st, :]).then_inc(norm_moments, 1)

            def moments_of(st):
                return moments[:, bass.ds(st, 1), 0:1].rearrange("p a b -> p (a b)")

            def rstd_of(st):
                return rstd[:, bass.ds(st, 1)]

            def normalize(st):
                dve.tensor_scalar(xn[:, st % 2, :], xres[:, st, :], moments[:, st, 0:1], rstd[:, st:st + 1],
                                  ALU.subtract, ALU.mult).then_inc(xn_ready, 1)

            def norm_lo(n0, st):
                dve.wait_ge(xT_hi_ready, n0 + st + 1)
                dve.tensor_tensor(xT_lo[:, :, st * P:(st + 1) * P],
                                  ps[:, 6 + st % 2, :].rearrange("p (k s) -> p k s", k=KT),
                                  xT_hi[:, :, st * P:(st + 1) * P].bitcast(F32), ALU.subtract).then_inc(xT_ready, 1)

            def norm_tiles(n0, half):
                tiles = range(half * HT, (half + 1) * HT)
                normalize(tiles[0])
                for st in tiles:
                    if st + 1 in tiles:
                        normalize(st + 1)
                    norm_lo(n0, st)

            dve.sem_inc(merged, MERGES)
            dve.sem_inc(lo_ready, 1)
            dve.sem_inc(hid_done, CREDIT)
            dve.sem_inc(qkv_taken, CREDIT)
            dve.sem_inc(k_rope, 1)
            dve.wait_ge(x_loaded[0], 16)
            norm_statistics(0, 0)
            clamp_codes(0, 0)
            dve.wait_ge(x_loaded[1], 16)
            norm_statistics(0, 1)
            dve.wait_ge(rstd_ready, 1)
            normalize(0)
            normalize(1)
            merge_first(0)
            norm_lo(0, 0)
            normalize(2)
            norm_lo(0, 1)
            normalize(3)
            merge_last(0, 0)
            norm_lo(0, 2)
            norm_lo(0, 3)
            clamp_codes(1, 1)
            dve.wait_ge(rstd_ready, 2)
            norm_tiles(0, 1)
            split_lo(0, 0)
            merge_first(1)
            merge_last(1, 1)
            clamp_codes(2, 0)
            merge_first(2)
            merge_last(2, 0)
            with dve.Fori(0, MT // 2 - 1) as i:
                for w in range(2):
                    s, u = 2 * i + 1 + w, (1 + w) % 2
                    split_lo(s, u)
                    clamp_codes(s + 2, u)
                    merge_first(s + 2)
                    hidden(0, s - 1, 0)
                    merge_last(s + 2, u)
                    hidden(0, s - 1, 1)
            for s in range(MT - 1, UNITS):
                u = s % 2
                split_lo(s, u)
                if s + 2 < UNITS:
                    clamp_codes(s + 2, u)
                    merge_first(s + 2)
                if s <= MT:
                    hidden(0, s - 1, 0)
                if s + 2 < UNITS:
                    merge_last(s + 2, u)
                if s <= MT:
                    hidden(0, s - 1, 1)
            for p in range(DU):
                v = UNITS + p
                hs_lo(dve, DU + p + 1, v % 2, 1, p, hs_ready)
                if p == 0:
                    add_down(0, 0)
                if p == 1:
                    dve.wait_ge(x_updated, HT)
                    norm_statistics(ST, 0)
                if p >= DU - KT:
                    c = p - (DU - KT)
                    dve.wait_ge(raw_hi, c + 1)
                    dve.tensor_tensor(wqkv[1][:, c, :], raw_w[:, c, :], wqkv[0][:, c, :].bitcast(F32), ALU.subtract
                                      ).then_inc(raw_split, 1)

            def normalize_tile(st, u):
                dve.tensor_scalar(xn[:, u, :], xres[:, bass.ds(st, 1), :].rearrange("p a e -> p (a e)"),
                                  moments_of(st), rstd_of(st), ALU.subtract, ALU.mult).then_inc(xn_ready, 1)

            def tile_lo(st, u):
                dve.wait_ge(xT_hi_ready, ST + st + 1)
                dve.tensor_tensor(xs[1][:, u, :, :], ps[:, 6 + u, :].rearrange("p (k s) -> p k s", k=KT),
                                  xs[0][:, u, :, :].bitcast(F32), ALU.subtract).then_inc(xT_ready, 1)

            def take_qkv(st, u):
                dve.wait_ge(xs_used, st + 1 + CREDIT)
                dve.wait_ge(q_rope, 3 * st + 1)
                dve.tensor_tensor(q_biased[:, :], ps[:, 3 * u, :], qkv_bias[:, 0:E], ALU.add).then_inc(qk_biased, 1)
                dve.tensor_tensor(k_biased[:, :], ps[:, 3 * u + 1, :], qkv_bias[:, E:2 * E], ALU.add).then_inc(qk_biased, 1)
                dve.tensor_tensor(v_nat[:, bass.ds(st, 1), :].rearrange("p a e -> p (a e)"), ps[:, 3 * u + 2, :],
                                  qkv_bias[:, 2 * E:3 * E], ALU.add).then_inc(qkv_taken, 1)
                rope(dve, k_nat, k_biased, k_swapped, st, (qk_biased, 2 * st + 2), k_rope)

            dve.wait_ge(rstd_ready, 3)
            normalize_tile(0, 0)
            normalize_tile(1, 1)
            add_down(1, 1)
            tile_lo(0, 0)
            dve.wait_ge(x_updated, ST)
            norm_statistics(ST, 1)
            dve.wait_ge(rstd_ready, 4)
            dve.wait_ge(consts_loaded, 16 * CONSTS)
            with dve.Fori(0, ST // 2 - 1) as i:
                for u in range(2):
                    st = 2 * i + u
                    normalize_tile(st + 2, u)
                    tile_lo(st + 1, 1 - u)
                    take_qkv(st, u)
            tile_lo(ST - 1, 1)
            take_qkv(ST - 2, 0)
            take_qkv(ST - 1, 1)

            dve.wait_ge(xs_used, ST + CREDIT)
            dve.wait_ge(pads_set, 7)
            dve.memset(maxima[:, :, :, :], -3.0e38).then_inc(maxima_set, 1)
            dve.wait_ge(maxima_set, 1)

            def attend(plan, g, u):
                side = 0
                for kind, n, rel in plan:
                    bank = SIDE_BANK + side % SIDE_BANKS
                    if kind == "stack":
                        kg = k_nat[:, :, bass.ds((g + 1) * GW, GW)].rearrange("p t (j d) -> p t j d", j=GH)
                        dve.wait_ge(stack_hi, 2 * (g + 1) + 1)
                        dve.tensor_copy(stack_k[:, :, :, D:2 * D], stack_k[:, :, :, 0:D]).then_inc(k_stacked, 1)
                        dve.tensor_tensor(stack_k[:, :, :, 2 * D:3 * D], kg, stack_k[:, :, :, 0:D], ALU.subtract
                                          ).then_inc(k_stacked, 1)
                    if kind == "stage_v":
                        if not leading(g):
                            dve.wait_ge(pv_done, NPV * g + CREDIT)
                        dve.tensor_copy(v_ext[1 - u][:, :, :, 0:D],
                                        v_nat[:, :, bass.ds((g + 1) * GW, GW)].rearrange("p t (j d) -> p t j d", j=GH)
                                        ).then_inc(v_staged, 1)
                    if kind == "turn" and side_engine(kind, n) == "dve":
                        dve.wait_ge(side_ready, sides_before(g) + side + 1)
                        take_turn(nc.vector, n, 1 - u if rel else u, bank)
                    if kind == "max":
                        st, c, width, heads = MAX_TILES[n]
                        dve.wait_ge(side_ready, sides_before(g) + side + 1)
                        dve.tensor_reduce(maxima[:, c // BANK, st, heads[0]:heads[-1] + 1:2],
                                          ps[:, bank, 0:len(heads) * width].rearrange("p (j n) -> p j n", n=width),
                                          AX.X, ALU.max).then_inc(side_taken["dve"], 1)
                    if kind == "stack_max":
                        tiles = slice(n * HT, (n + 1) * HT)
                        dve.wait_ge(side_taken["dve"], sides_before(g, "dve") + sides_of(plan)[:side].count("dve"))
                        dve.tensor_tensor(row_max[:, tiles, :], maxima[:, 0, tiles, :], maxima[:, 1, tiles, :], ALU.max
                                          ).then_inc(row_max_step, 1)
                        dve.wait_ge(row_max_step, 2 * (g + rel) + n + 1)
                        dve.tensor_scalar(stack_q[:, tiles, :, KA].bitcast(F32R), row_max[:, tiles, :], -1.0, None,
                                          ALU.mult).then_inc(max_stacked, 1)
                        dve.wait_ge(max_stacked, 4 * (g + rel) + 2 * n + 1)
                        dve.scalar_tensor_tensor(stack_q[:, tiles, :, KA + 1], row_max[:, tiles, :], -1.0,
                                                 stack_q[:, tiles, :, KA], ALU.mult, ALU.subtract
                                                 ).then_inc(max_stacked, 1)
                    if kind == "turn_ctx":
                        gc = g + rel
                        dve.wait_ge(side_ready, sides_before(g) + side + 1)
                        tile = ps[:, bank, :].rearrange("p (t j d) -> p t j d", t=HT, j=GH)
                        dve.reciprocal(inv_den[:, n, :, :], tile[:, :, :, D]).then_inc(inverted, 1)
                        dve.wait_ge(inverted, 2 * gc + n + 1)
                        dve.tensor_tensor(ctx_nat[:, n * HT:(n + 1) * HT, bass.ds(gc * GW, GW)]
                                          .rearrange("p t (j d) -> p t j d", j=GH), tile[:, :, :, 0:D],
                                          inv_den[:, n, :, :].unsqueeze(3).broadcast_to([P, HT, GH, D]), ALU.mult
                                          ).then_inc(side_taken["dve"], 1)
                    if kind in SIDE_KINDS:
                        side += 1

            run_groups(dve, attend)

            dve.sem_inc(ctx_lo, CREDIT)
            dve.sem_inc(x_attended, CREDIT)

            def ctx_low(st):
                u = st % 2
                dve.wait_ge(ctx_hi, st + 1)
                dve.tensor_tensor(xs[1][:, u, :, :], ps[:, 2 + u, :].rearrange("p (k s) -> p k s", k=KT),
                                  xs[0][:, u, :, :].bitcast(F32), ALU.subtract).then_inc(ctx_lo, 1)

            def add_attended(st):
                dve.wait_ge(projected, st + 1 + CREDIT)
                dve.tensor_tensor(xres[:, st, :], xres[:, st, :], ps[:, st % 2, :], ALU.add).then_inc(x_attended, 1)
                dve.wait_ge(x_attended, st + 1 + CREDIT)
                dve.bn_stats(stats[:, st, :], xres[:, st, :]).then_inc(norm_stats, 1)
                dve.wait_ge(norm_stats, 2 * ST + st + 1)
                dve.bn_aggr(moments[:, st, :], stats[:, st, :]).then_inc(norm_moments, 1)

            dve.wait_ge(bias_added, ST)
            ctx_low(0)
            for st in range(ST - 1):
                ctx_low(st + 1)
                add_attended(st)
                if st == HT:
                    dve.wait_ge(rstd_ready, 5)
                    normalize(0)
                    normalize(1)
                if st > HT:
                    norm_lo(2 * ST, st - HT - 1)
                    normalize(st - HT + 1)
            add_attended(ST - 1)

            norm_lo(2 * ST, 2)
            norm_lo(2 * ST, 3)
            dve.wait_ge(rstd_ready, 6)
            norm_tiles(2 * ST, 1)
            def hs_low(q, p):
                n = MT + DU * q + p
                hs_lo(dve, DU * (2 + q) + p + 1, n % 2, 1 - q, p, hs_ready)

            with dve.Fori(0, MT - 1) as mt:
                for half in range(2):
                    hidden(1, mt, half)
            hs_low(0, 0)
            hs_low(0, 1)
            for half in range(2):
                hidden(1, MT - 1, half)
            for p in range(2, DU):
                hs_low(0, p)
            for p in range(DU):
                hs_low(1, p)
                if p == 0:
                    add_down(2, 1)
            add_down(3, 0)

        @block.tensor
        def _(pe):
            def turn(s, src):
                pe.wait_ge(w_ready, s + 1)
                pe.wait_ge(lo_ready, s + 1)
                for b in range(8):
                    ins = pe.transpose(ps[:, 4 + b // 4, (b % 4) * P:(b % 4 + 1) * P], src(b), ident[:, :])
                ins.then_inc(w_turned, 1)

            def turn_gate_up(s):
                turn(s, lambda b: w_scaled[:, b * P:(b + 1) * P])

            def turn_down(s):
                wv = w_scaled[:, :].rearrange("p (c m) -> p c m", c=KT)
                turn(s, lambda b: wv[:, b % 4, (b // 4) * P:(b // 4 + 1) * P])

            def weights_ready(v, u, k):
                if k is None:
                    pe.wait_ge(lo_ready, v + 2)
                else:
                    pe.wait_ge(reloaded[u], 16 * k)

            def gate_up(call, mt, v, u, k=None, halves=(0, 1), parts=(0, 1)):
                weights_ready(v, u, k)
                for half in halves:
                    cols = slice(half * HALF, (half + 1) * HALF)
                    pe.wait_ge(hid_done, 2 * MT * call + 2 * mt + half + 1)
                    for g in parts:
                        bank = ps[:, 2 * half + g, :]
                        for kt in range(KT):
                            w = [wT[u][:, part, (4 * g + kt) * P:(4 * g + kt + 1) * P] for part in range(2)]
                            pe.matmul(bank, w[0], xT_hi[:, kt, cols], start=kt == 0, stop=False)
                            pe.matmul(bank, w[1], xT_hi[:, kt, cols], start=False, stop=False)
                            ins = pe.matmul(bank, w[0], xT_lo[:, kt, cols], start=False, stop=kt == KT - 1)
                        ins.then_inc((gate_done, up_done)[g], 1)

            def down(half, v, u, h, k, first, last):
                weights_ready(v, u, k)
                if h <= DU:
                    pe.wait_ge(first_hs_ready, h)
                else:
                    pe.wait_ge(hs_ready, h - DU)
                for j in range(2):
                    for t in range(HT):
                        a = [hs[u][:, part, j, t * P:(t + 1) * P] for part in range(2)]
                        w = [wT[u][:, part, j * E:(j + 1) * E] for part in range(2)]
                        bank = ps[:, 4 * half + t, :]
                        pe.matmul(bank, a[0], w[0], start=first and j == 0, stop=False)
                        pe.matmul(bank, a[1], w[0], start=False, stop=False)
                        ins = pe.matmul(bank, a[0], w[1], start=False, stop=last and j == 1)
                ins.then_inc(down_used, 1)

            def norm_turn(n):
                pe.wait_ge(xn_ready, n + 1)
                if n >= 2:
                    pe.wait_ge(xT_ready, n - 1)
                for k in range(KT):
                    ins = pe.transpose(ps[:, 6 + n % 2, k * P:(k + 1) * P], xn[:, n % 2, k * P:(k + 1) * P], ident[:, :])
                ins.then_inc(xn_turned, 1)

            pe.sem_inc(w_turned, 1)
            pe.sem_inc(up_done, 4)
            pe.wait_ge(first_loaded, 16 * FIRST_CONSTS)
            for st in range(ST):
                norm_turn(st)
            turn_gate_up(0)
            pe.wait_ge(xT_ready, ST)
            gate_up(0, 0, 0, 0)
            turn_gate_up(1)
            gate_up(0, 1, 1, 1, halves=[0])
            turn_gate_up(2)
            gate_up(0, 1, 1, 1, halves=[1])
            with pe.Fori(0, MT // 2 - 2) as i:
                for w in range(2):
                    s, u = 2 * i + 3 + w, (1 + w) % 2
                    turn_gate_up(s)
                    gate_up(0, s - 1, s - 1, 1 - u)
            for s in range(MT - 1, UNITS):
                (turn_gate_up if s < MT else turn_down)(s)
                if s <= MT:
                    gate_up(0, s - 1, s - 1, (s - 1) % 2)
                else:
                    if s == MT + 1:
                        pe.wait_ge(hid_done, 2 * MT + CREDIT)
                    down(0, s - 1, (s - 1) % 2, s - MT, None, s == MT + 1, False)
            down(0, UNITS - 1, (UNITS - 1) % 2, DU, None, False, True)
            for p in range(DU):
                v = UNITS + p
                down(1, v, v % 2, DU + p + 1, reload_count(v), p == 0, p == DU - 1)

            pe.sem_inc(xs_used, CREDIT)
            pe.sem_inc(pv_done, CREDIT)

            def project(u, w, cols, banks, done):
                for b in range(cols // BANK):
                    c = slice(b * BANK, (b + 1) * BANK)
                    for kt in range(KT):
                        pe.matmul(ps[:, banks + b, :], xs[0][:, u, kt, :], w[0][:, kt, c], start=kt == 0, stop=False)
                        pe.matmul(ps[:, banks + b, :], xs[1][:, u, kt, :], w[0][:, kt, c], start=False, stop=False)
                        ins = pe.matmul(ps[:, banks + b, :], xs[0][:, u, kt, :], w[1][:, kt, c], start=False,
                                        stop=kt == KT - 1)
                ins.then_inc(done, 1)

            def turn_tile(st, u):
                pe.wait_ge(xn_ready, ST + st + 1)
                pe.wait_ge(xT_ready, ST + st - 1)
                for k in range(KT):
                    ins = pe.transpose(ps[:, 6 + u, k * P:(k + 1) * P], xn[:, u, k * P:(k + 1) * P], ident[:, :])
                ins.then_inc(xn_turned, 1)

            def project_qkv(st, u):
                pe.wait_ge(xT_ready, ST + st + 1)
                pe.wait_ge(qkv_taken, st + 1)
                project(u, wqkv, 3 * E, 3 * u, xs_used)

            pe.wait_ge(x_updated, HT + 2)
            turn_tile(0, 0)
            pe.wait_ge(raw_split, KT)
            pe.wait_ge(x_updated, ST)
            with pe.Fori(0, ST // 2 - 1) as i:
                for u in range(2):
                    turn_tile(2 * i + u + 1, 1 - u)
                    project_qkv(2 * i + u, u)
            turn_tile(ST - 1, 1)
            project_qkv(ST - 2, 0)
            project_qkv(ST - 1, 1)

            pe.wait_ge(qkv_taken, ST + CREDIT)
            pe.wait_ge(const_set, 4)

            def attend(plan, g, u):
                side = 0
                order = sides_of(plan)

                def wait_taken(engine, count):
                    pe.wait_ge(side_taken[engine], sides_before(g, engine) + count)

                def wait_side_bank():
                    if side >= SIDE_BANKS:
                        last = side - SIDE_BANKS
                        wait_taken(order[last], order[:last + 1].count(order[last]))
                    elif side == 0 and not leading(g):
                        for engine in side_taken:
                            wait_taken(engine, 0)

                def wait_turns(names, rel):
                    at = [k for k, (kind, n, r) in enumerate(e for e in plan if e[0] in SIDE_KINDS)
                          if kind == "turn" and r == rel and TURNS[n] in names]
                    for engine in side_taken:
                        last = [k for k in at if order[k] == engine]
                        if last:
                            wait_taken(engine, order[:last[-1] + 1].count(engine))

                for kind, n, rel in plan:
                    bank = SIDE_BANK + side % SIDE_BANKS
                    if kind == "turn":
                        operand, pair, half = TURNS[n]
                        if operand == "k":
                            pe.wait_ge(k_stacked, 2 * (g + 2))
                        elif operand == "q":
                            pe.wait_ge(q_stacked, 2 * (g + 2))
                        else:
                            pe.wait_ge(max_stacked, 4 * (g + rel) + 2 * half + 2)
                        wait_side_bank()
                        stack = stack_k if operand == "k" else stack_q
                        for t in range(HT):
                            src = stack[:, half * HT + t, 2 * pair:2 * pair + 2, :].rearrange("p j d -> p (j d)")
                            ins = pe.transpose(ps[:, bank, t * P:(t + 1) * P], src, ident[:, :])
                        ins.then_inc(side_ready, 1)
                    if kind == "max":
                        st, c, width, heads = MAX_TILES[n]
                        if n == 0:
                            wait_turns([(operand, pair, 0) for operand in "kq" for pair in range(2)], 1)
                        if n == NMAX_LOW:
                            wait_turns([(operand, pair, 1) for operand in "kq" for pair in range(2)], 1)
                        wait_side_bank()
                        diagonal = c + width == (st + 1) * P
                        for h, j in enumerate(heads):
                            rows = slice(j % 2 * SLOT, j % 2 * SLOT + KA)
                            end = (h + 1) * width
                            ins = pe.matmul(ps[:, bank, end - width:end], qT[rows, j // 2, st * P:(st + 1) * P],
                                            kT[1 - u if rel else u][rows, j // 2, c:c + width], start=True, stop=not diagonal,
                                            tile_position=(j % 2 * SLOT, 0))
                            if diagonal:
                                ins = pe.matmul(ps[:, bank, end - P:end], ident_bf16[:, :], causal_mask[:, :],
                                                start=False, stop=True)
                        ins.then_inc(side_ready, 1)
                    if kind == "score":
                        half, kt = PV_STEPS[n // 2]
                        c = first_col(half, kt)
                        pair = n % 2
                        if n == 0:
                            for engine in side_taken:
                                wait_taken(engine, 0)
                        if n == 2 * HT:
                            wait_turns([("m", pair, 1) for pair in range(2)], 0)
                        pe.wait_ge(exp_done, 2 * NPV * g + n + 1)
                        for j in range(2):
                            rows = slice(j * SLOT, j * SLOT + KB)
                            ins = pe.matmul(ps[:, 2 * pair + j, c:HALF], kT[u][rows, pair, kt * P:(kt + 1) * P],
                                            qTm[u][rows, pair, half * HALF + c:(half + 1) * HALF], start=True, stop=True,
                                            tile_position=(j * SLOT, 0))
                        ins.then_inc(scored, 1)
                    if kind == "pv":
                        half, kt = PV_STEPS[n]
                        c = first_col(half, kt)
                        gc, uc = g + rel, u if rel == 0 else 1 - u
                        if n == 0:
                            pe.wait_ge(v_staged, gc + 1)
                        if kt == 0:
                            pe.wait_ge(ctxT_taken, 2 * gc + half + 1)
                        if DIAG[n]:
                            pe.wait_ge(diag_masked, 2 * NDIAG * gc + 2 * sum(DIAG[:n + 1]))
                        pe.wait_ge(exp_done, 2 * NPV * gc + 2 * n + 2 + CREDIT)
                        for j in range(GH):
                            ins = pe.matmul(ps[32 * j:32 * (j + 1), PV_BANK, c:HALF], v_ext[uc][:, kt, j, :],
                                            probs[n % 2][j // 2][:, j % 2, c:HALF], start=kt == 0,
                                            stop=n in (HT - 1, NPV - 1), tile_position=(0, 32 * j))
                        ins.then_inc(pv_done, 1)
                    if kind == "turn_ctx":
                        pe.wait_ge(ctxT_taken, 2 * (g + rel) + n + 2)
                        wait_side_bank()
                        for t in range(HT):
                            ins = pe.transpose(ps[:, bank, t * P:(t + 1) * P], ctxT[:, t * P:(t + 1) * P], ident[:, :])
                        ins.then_inc(side_ready, 1)
                    if kind in SIDE_KINDS:
                        side += 1

            run_groups(pe, attend)

            def turn_ctx_tile(st, u):
                pe.wait_ge(ctx_lo, st + 1)
                for k in range(KT):
                    ins = pe.transpose(ps[:, 2 + u, k * P:(k + 1) * P], ctx_nat[:, st, k * P:(k + 1) * P], ident[:, :])
                ins.then_inc(ctx_turned, 1)

            pe.wait_ge(side_taken["dve"], sides_before(GROUPS, "dve") + 1)
            pe.wait_ge(wo_split, KT)
            def project_context(st, u):
                pe.wait_ge(ctx_lo, st + 1 + CREDIT)
                pe.wait_ge(x_attended, st + 1)
                project(u, wo, E, u, projected)

            pe.sem_inc(projected, CREDIT)
            turn_ctx_tile(0, 0)
            for st in range(ST):
                if st + 1 < ST:
                    turn_ctx_tile(st + 1, (st + 1) % 2)
                project_context(st, st % 2)
                if st > HT:
                    norm_turn(2 * ST + st - HT - 1)

            norm_turn(2 * ST + HT - 1)
            pe.wait_ge(xT_ready, 2 * ST + HT)
            pe.wait_ge(x_attended, ST + CREDIT)
            for g in range(2):
                gate_up(1, 0, 0, 0, reload_count(CALL_UNITS), halves=[0], parts=[g])
                for st in (HT + 2 * g, HT + 2 * g + 1):
                    norm_turn(2 * ST + st)
            pe.wait_ge(xT_ready, 3 * ST)
            gate_up(1, 0, 0, 0, reload_count(CALL_UNITS), halves=[1])
            with pe.Fori(0, MT // 2 - 1) as i:
                for w in range(2):
                    mt, u = 2 * i + 1 + w, 1 - w
                    gate_up(1, mt, mt, u, i + reload_count(CALL_UNITS + 1 + w))
            gate_up(1, MT - 1, MT - 1, 1, reload_count(CALL_UNITS + MT - 1))
            for q in range(2):
                for p in range(DU):
                    n = MT + DU * q + p
                    down(1 - q, n, n % 2, DU * (2 + q) + p + 1, reload_count(CALL_UNITS + n), p == 0, p == DU - 1)


_INPUTS = ["L0_attn_hidden_states", "L0_attn_qkv_w", "L0_attn_qkv_b", "L0_attn_out_w", "L0_attn_out_b",
           "L0_ffn_gate_q", "L0_ffn_gate_absmax", "L0_ffn_up_q", "L0_ffn_up_absmax", "L0_ffn_down_q",
           "L0_ffn_down_absmax"]


def _constants(seq, head_dim):
    import numpy as np
    half = head_dim // 2
    inv_freq = np.float32(1.0) / np.float32(10000.0) ** (np.arange(half, dtype=np.float32) / np.float32(half))
    ang = np.arange(seq, dtype=np.float32)[:, None] * inv_freq[None, :].astype(np.float32)
    cos, sin = np.cos(ang).astype(np.float32), np.sin(ang).astype(np.float32)
    return {
        "rope_cos": np.concatenate([cos, cos], 1),
        "rope_sin": np.concatenate([-sin, sin], 1),
        "identity": np.eye(P, dtype=np.float32),
    }


def kernel(**inputs):
    import numpy as np
    import concourse.bacc as bacc
    from concourse.bass_utils import run_bass_kernel_spmd

    nc = bacc.Bacc("TRN2", target_bir_lowering=False, num_devices=1)
    shape = inputs["L0_attn_hidden_states"].shape
    named = [(n, np.ascontiguousarray(inputs[n])) for n in _INPUTS]
    named += list(_constants(shape[1], shape[2] // HEADS).items())
    arrays, args = {}, []
    for name, a in named:
        arrays[f"in_{name}"] = a
        args.append(nc.dram_tensor(f"in_{name}", a.shape, mybir.dt.from_np(a.dtype), kind="ExternalInput").ap())
    args.append(nc.dram_tensor("out_0", shape, F32, kind="ExternalOutput").ap())
    macaron_block(nc, *args)
    r = run_bass_kernel_spmd(nc, [arrays], core_ids=[0])
    return r.results[0]["out_0"]
```
